# Optimizing a Trainium2 kernel written in Bass

```python
import numpy as np
import jax
import jax.numpy as jnp

def _softmax(x, axis=-1):
    return jax.nn.softmax(x, axis=axis)

def _gelu(x):
    return jax.nn.gelu(x, approximate=True)

def _silu(x):
    return jax.nn.silu(x)

def _sigmoid(x):
    return jax.nn.sigmoid(x)

def _layernorm(x, axis=-1, eps=1e-05):
    m = jnp.mean(x, axis=axis, keepdims=True)
    v = jnp.var(x, axis=axis, keepdims=True)
    return (x - m) / jnp.sqrt(v + eps)

def _scatter_add(tgt, idx, src, axis=0):
    return tgt.at[idx].add(src)

def _segment_sum(src, seg, n):
    return jax.ops.segment_sum(src, seg, n)
kernel_name = 'mk_seq_postln_d1_jaxref_r8_f4312d'

def setup_inputs(seed: int=0):
    np.random.seed(seed)
    _w = jnp.asarray

    def _L0_attn_setup():
        import jax, jax.numpy as jnp
        import numpy as np
        import math
        N_HEAD = 16

        def sparsemax_lastdim(z):
            z_sorted = jnp.flip(jnp.sort(z, axis=-1), axis=-1)
            cs = jnp.cumsum(z_sorted, axis=-1)
            d = z.shape[-1]
            rho = jnp.arange(1, d + 1, dtype=z.dtype)
            support = 1.0 + rho * z_sorted > cs
            k = jnp.maximum(jnp.sum(support, axis=-1, keepdims=True), 1)
            cs_k = jnp.take_along_axis(cs, k - 1, axis=-1)
            tau = (cs_k - 1.0) / k.astype(z.dtype)
            return jnp.maximum(z - tau, 0.0)
        key = jax.random.key(seed)
        k1, k2, k3, k4, k5 = jax.random.split(key, 5)
        B, T, C = (2, 256, 128)
        x = jax.random.normal(k1, (B, T, C), dtype=jnp.float32)
        w_attn = jax.random.normal(k2, (C, 3 * C), dtype=jnp.float32) * (1.0 / math.sqrt(C))
        b_attn = jax.random.normal(k3, (3 * C,), dtype=jnp.float32) * 0.02
        w_proj = jax.random.normal(k4, (C, C), dtype=jnp.float32) * (1.0 / math.sqrt(C))
        b_proj = jax.random.normal(k5, (C,), dtype=jnp.float32) * 0.02
        return {'x': x, 'w_attn': w_attn, 'b_attn': b_attn, 'w_proj': w_proj, 'b_proj': b_proj}
    _L0_attn_in = _L0_attn_setup()

    def _L0_ffn_setup():
        import jax, jax.numpy as jnp
        import numpy as np
        NUM_EXPERTS = 8
        TOP_K = 2

        def _swiglu(x, w1, w2, w3):
            return jax.nn.silu(x @ w1) * (x @ w3) @ w2
        key = jax.random.key(seed)
        ks = jax.random.split(key, 9)
        B, S, D, H, E = (1, 128, 128, 128, NUM_EXPERTS)
        std = 0.02
        return {'x': jax.random.normal(ks[0], (B, S, D), jnp.float32), 'router_w': jax.random.normal(ks[1], (D, E), jnp.float32) * std, 'expert_bias': jnp.zeros((E,), jnp.float32), 'w1': jax.random.normal(ks[2], (E, D, H), jnp.float32) * std, 'w2': jax.random.normal(ks[3], (E, H, D), jnp.float32) * std, 'w3': jax.random.normal(ks[4], (E, D, H), jnp.float32) * std, 'sw1': jax.random.normal(ks[5], (D, H), jnp.float32) * std, 'sw2': jax.random.normal(ks[6], (H, D), jnp.float32) * std, 'sw3': jax.random.normal(ks[7], (D, H), jnp.float32) * std}
    _L0_ffn_in = _L0_ffn_setup()
    _d = {'L0_attn_x': _L0_attn_in['x'], 'L0_attn_w_attn': _L0_attn_in['w_attn'], 'L0_attn_b_attn': _L0_attn_in['b_attn'], 'L0_attn_w_proj': _L0_attn_in['w_proj'], 'L0_attn_b_proj': _L0_attn_in['b_proj'], 'L0_ffn_router_w': _L0_ffn_in['router_w'], 'L0_ffn_expert_bias': _L0_ffn_in['expert_bias'], 'L0_ffn_w1': _L0_ffn_in['w1'], 'L0_ffn_w2': _L0_ffn_in['w2'], 'L0_ffn_w3': _L0_ffn_in['w3'], 'L0_ffn_sw1': _L0_ffn_in['sw1'], 'L0_ffn_sw2': _L0_ffn_in['sw2'], 'L0_ffn_sw3': _L0_ffn_in['sw3']}
    _x0 = _d['L0_attn_x']
    _d['L0_attn_x'] = jax.random.normal(jax.random.fold_in(jax.random.key(seed), 1), (8, 512, 128), dtype=_x0.dtype)
    del _x0
    return _d

def reference(L0_attn_x, L0_attn_w_attn, L0_attn_b_attn, L0_attn_w_proj, L0_attn_b_proj, L0_ffn_router_w, L0_ffn_expert_bias, L0_ffn_w1, L0_ffn_w2, L0_ffn_w3, L0_ffn_sw1, L0_ffn_sw2, L0_ffn_sw3):

    def _L0_attn_ref(x, w_attn, b_attn, w_proj, b_proj):
        import jax, jax.numpy as jnp
        import numpy as np
        import math
        N_HEAD = 16

        def sparsemax_lastdim(z):
            z_sorted = jnp.flip(jnp.sort(z, axis=-1), axis=-1)
            cs = jnp.cumsum(z_sorted, axis=-1)
            d = z.shape[-1]
            rho = jnp.arange(1, d + 1, dtype=z.dtype)
            support = 1.0 + rho * z_sorted > cs
            k = jnp.maximum(jnp.sum(support, axis=-1, keepdims=True), 1)
            cs_k = jnp.take_along_axis(cs, k - 1, axis=-1)
            tau = (cs_k - 1.0) / k.astype(z.dtype)
            return jnp.maximum(z - tau, 0.0)
        B, T, C = x.shape
        H = N_HEAD
        hd = C // H
        qkv = x @ w_attn + b_attn
        q, k, v = jnp.split(qkv, 3, axis=-1)
        q = q.reshape(B, T, H, hd).transpose(0, 2, 1, 3)
        k = k.reshape(B, T, H, hd).transpose(0, 2, 1, 3)
        v = v.reshape(B, T, H, hd).transpose(0, 2, 1, 3)
        att = jnp.einsum('bhqd,bhkd->bhqk', q, k) * (1.0 / math.sqrt(hd))
        causal = jnp.tril(jnp.ones((T, T), dtype=bool))
        att = jnp.where(causal[None, None], att, -jnp.inf)
        att = sparsemax_lastdim(att)
        y = jnp.einsum('bhqk,bhkd->bhqd', att, v)
        y = y.transpose(0, 2, 1, 3).reshape(B, T, C)
        return y @ w_proj + b_proj

    def _L0_ffn_ref(x, router_w, expert_bias, w1, w2, w3, sw1, sw2, sw3):
        import jax, jax.numpy as jnp
        import numpy as np
        NUM_EXPERTS = 8
        TOP_K = 2

        def _swiglu(x, w1, w2, w3):
            return jax.nn.silu(x @ w1) * (x @ w3) @ w2
        B, S, D = x.shape
        E, K = (NUM_EXPERTS, TOP_K)
        N = B * S
        x_flat = x.reshape(N, D)
        logits = x_flat @ router_w
        scores = jax.nn.softmax(logits.astype(jnp.float32), axis=-1)
        _, sel = jax.lax.top_k(scores + expert_bias[None, :], K)
        top_scores = jnp.take_along_axis(scores, sel, axis=-1)
        flat_exp = sel.reshape(-1)
        order = jnp.argsort(flat_exp)
        exp_sorted = flat_exp[order]
        routed_input = x_flat[order // K]
        routed_output = jnp.zeros_like(routed_input)
        for e in range(E):
            mask = (exp_sorted == e)[:, None]
            y_e = _swiglu(routed_input, w1[e], w2[e], w3[e])
            routed_output = routed_output + jnp.where(mask, y_e, 0.0)
        unsorted = jnp.zeros((N * K, D), routed_output.dtype).at[order].set(routed_output)
        unsorted = unsorted.reshape(N, K, D)
        out_experts = jnp.einsum('nk,nkd->nd', top_scores, unsorted)
        shared_out = _swiglu(x_flat, sw1, sw2, sw3)
        return (shared_out + out_experts).reshape(B, S, D)
    x = L0_attn_x
    x = _layernorm(x + _L0_attn_ref(x, L0_attn_w_attn, L0_attn_b_attn, L0_attn_w_proj, L0_attn_b_proj), axis=-1)
    x = _layernorm(x + _L0_ffn_ref(x, L0_ffn_router_w, L0_ffn_expert_bias, L0_ffn_w1, L0_ffn_w2, L0_ffn_w3, L0_ffn_sw1, L0_ffn_sw2, L0_ffn_sw3), axis=-1)
    return x

_drawn_inputs = setup_inputs


def setup_inputs(seed=0):
    import zlib

    import numpy as np

    out = dict(_drawn_inputs(seed))
    spreads = {'L0_ffn_expert_bias': (0.0, 0.8)}
    factors = {'L0_attn_b_proj': 3.378,
     'L0_ffn_router_w': 8.0,
     'L0_ffn_w1': 8.0,
     'L0_ffn_w2': 8.0,
     'L0_ffn_w3': 8.0,
     'L0_ffn_sw1': 8.0,
     'L0_ffn_sw2': 8.0,
     'L0_ffn_sw3': 8.0}
    for name, (base, spread) in spreads.items():
        noise = np.random.default_rng([zlib.crc32(name.encode()), seed]).standard_normal(out[name].shape)
        drawn = base * np.exp(spread * noise) if base else spread * noise
        out[name] = jnp.asarray(drawn.astype(out[name].dtype))
    for name, factor in factors.items():
        out[name] = (out[name] * factor).astype(out[name].dtype)
    return out
```

```python
import concourse.bass as bass
from concourse import mybir
from contextlib import ExitStack

F32 = mybir.dt.float32
BF16 = mybir.dt.bfloat16
I32 = mybir.dt.int32
ALU = mybir.AluOpType
ACT = mybir.ActivationFunctionType
AX = mybir.AxisListType.X

B, T, C = 8, 512, 128
H = 16
HD = C // H
P = 128
QT = T // P
NT = B * QT
NE = 8
PARTS = 3
KROWS = PARTS * PARTS * HD
KTAU = KROWS + PARTS
ROWSETS = H * QT
CH = 4
TOP = 8
MASKED = -1e30
EPS = 1e-5
SBANKS = 4
NEWTON = 24
FEW = 3
CLOSE = 3e-6
JOBS = 40
SCALE = 1.0 / float(HD) ** 0.5


class Batch:

    def __init__(self, n):
        self.n, self.pair, self.p = n, n // 2, n % 2


BATCHES = [Batch(n) for n in range(B)]


def wait(eng, sem, n, per, more):
    if n * per + more > 0:
        eng.wait_ge(sem, n * per + more)


def setup_and_projections(nc, x, w_attn, b_attn, q_parts, k_parts, ident, ident16, mask_q, mask_k,
                          ones, v_all):
    with ExitStack() as ctx:
        def sb(name, shape, dt=F32):
            return ctx.enter_context(nc.sbuf_tensor(name, shape, dt))

        def sem(name):
            return ctx.enter_context(nc.semaphore(name))

        w_sb = sb("w_sb", [P, 3 * C])
        bias_qk = sb("bias_qk", [P, 2])
        bias_v = sb("bias_v", [1, C])
        x_in = [sb(f"x_in{i}", [P, QT, C]) for i in range(2)]
        x_t = [sb(f"x_t{i}", [P, T]) for i in range(2)]
        full = [[sb(f"full{j}{i}", [P, T]) for i in range(2)] for j in range(2)]
        parts = [[sb(f"parts{j}{i}", [P, PARTS, T], BF16) for i in range(2)] for j in range(2)]
        rest = [[sb(f"rest{j}{i}", [P, T]) for i in range(2)] for j in range(2)]
        xt_ps = [ctx.enter_context(nc.psum_tensor(f"xt_ps{i}", [P, T], F32)) for i in range(2)]
        qk_ps = [[ctx.enter_context(nc.psum_tensor(f"qk_ps{j}{i}", [P, T], F32)) for i in range(2)]
                 for j in range(2)]
        v_ps = [ctx.enter_context(nc.psum_tensor(f"v_ps{i}", [P, T], F32)) for i in range(2)]

        weights_in = sem("weights_in")
        x_loaded = [sem(f"x_loaded{i}") for i in range(2)]
        consts = sem("consts")
        consts2 = sem("consts2")
        xt_ready = sem("xt_ready")
        xt_copied = sem("xt_copied")
        qk_ready = sem("qk_ready")
        v_ready = sem("v_ready")
        v_copied = sem("v_copied")
        act_done = sem("act_done")
        rest_done = sem("rest_done")
        second_done = sem("second_done")
        third_done = sem("third_done")
        bias_scaled = sem("bias_scaled")
        stored = [sem(f"stored{i}") for i in range(2)]
        block = ctx.enter_context(nc.Block())

        @block.gpsimd
        def _(pool):
            nc.gpsimd.memset(ident[:], 0.0).then_inc(consts, 1)
            nc.gpsimd.memset(mask_q[:], 0.0).then_inc(consts, 1)
            nc.gpsimd.memset(mask_k[:], 0.0).then_inc(consts, 1)
            nc.gpsimd.memset(ones[:], 1.0).then_inc(consts, 1)
            pool.wait_ge(consts, 4)
            nc.gpsimd.affine_select(out=ident[:], in_=ident[:], compare_op=ALU.not_equal, fill=1.0,
                                    base=0, pattern=[[-1, P]], channel_multiplier=1).then_inc(consts, 1)
            nc.gpsimd.affine_select(out=mask_q[:], in_=mask_q[:], compare_op=ALU.is_ge, fill=MASKED,
                                    base=T - P, pattern=[[-1, 2 * T - P]],
                                    channel_multiplier=1).then_inc(consts, 1)
            nc.gpsimd.affine_select(out=mask_k[:], in_=mask_k[:], compare_op=ALU.is_ge, fill=MASKED,
                                    base=0, pattern=[[1, P]], channel_multiplier=-1).then_inc(consts, 1)
            pool.wait_ge(consts, 7)
            nc.gpsimd.tensor_copy(ident16[:], ident[:]).then_inc(consts2, 1)

        @block.sync
        def _(sp):
            def load(b):
                sp.dma_start(x_in[b.p][:], x[b.n].rearrange("(t p) c -> p t c", p=P)
                             ).then_inc(x_loaded[b.p], 16)

            load(BATCHES[0])
            sp.dma_start(w_sb[:], w_attn).then_inc(weights_in, 16)
            sp.dma_start(bias_qk[:], b_attn[0:2 * C].rearrange("(j p) -> p j", p=P),
                         allow_slow_non_contiguous=True).then_inc(weights_in, 16)
            sp.dma_start(bias_v[:], b_attn[2 * C:3 * C].rearrange("(a n) -> a n", a=1)).then_inc(weights_in, 16)
            load(BATCHES[1])

            def store(b):
                wait(sp, third_done, b.n, 2, 2)
                for j, dst in enumerate((q_parts, k_parts)):
                    for i in range(PARTS):
                        to = bass.AP(dst.tensor, (b.n * PARTS + i) * (C * T), [[T, H], [H * T, HD], [1, T]])
                        sp.dma_start(to, parts[j][b.p][:, i, :]).then_inc(stored[b.p], 16)
                if b.n + 2 < B:
                    load(BATCHES[b.n + 2])

            for b in BATCHES:
                store(b)
            for p in range(2):
                sp.wait_ge(stored[p], 96 * (B // 2))

        @block.tensor
        def _(pe):
            pe.wait_ge(consts, 7)
            pe.wait_ge(weights_in, 48)

            def step(b):
                p = b.p
                wait(pe, x_loaded[p], b.pair, 16, 16)
                wait(pe, xt_copied, b.n, 1, 1)
                for t in range(QT):
                    last = nc.tensor.transpose(xt_ps[p][:, t * P:(t + 1) * P], x_in[p][:, t, :], ident[:])
                last.then_inc(xt_ready, 1)
                wait(pe, xt_copied, b.n, 1, 3)
                wait(pe, act_done, b.n, 6, 4)
                for j in range(2):
                    nc.tensor.matmul(qk_ps[j][p][:], w_sb[:, j * C:(j + 1) * C], x_t[p][:],
                                     start=True, stop=True).then_inc(qk_ready, 1)
                wait(pe, v_copied, b.n, 1, 0)
                nc.tensor.matmul(v_ps[p][:], ones[0:1, :], bias_v[0:1, :].unsqueeze(1).broadcast_to([1, QT, C]),
                                 start=True, stop=False)
                for t in range(QT):
                    last = nc.tensor.matmul(v_ps[p][:, t * P:(t + 1) * P], x_t[p][:, t * P:(t + 1) * P],
                                            w_sb[:, 2 * C:3 * C], start=False, stop=t == QT - 1)
                last.then_inc(v_ready, 1)

            for b in BATCHES:
                step(b)

        @block.scalar
        def _(act):
            act.wait_ge(weights_in, 48)
            nc.scalar.mul(bias_qk[:, 0:1], bias_qk[:, 0:1], SCALE).then_inc(bias_scaled, 1)
            act.wait_ge(bias_scaled, 1)
            act.sem_inc(xt_copied, 2)
            act.sem_inc(act_done, 12)

            def step(b):
                p = b.p
                wait(act, xt_ready, b.n, 1, 1)
                wait(act, v_ready, b.n, 1, 0)
                nc.scalar.copy(x_t[p][:], xt_ps[p][:]).then_inc(xt_copied, 1)
                for j in range(2):
                    wait(act, qk_ready, b.n, 2, j + 1)
                    wait(act, rest_done, b.n, 2, 0)
                    if j == 0:
                        wait(act, stored[p], b.pair, 96, 0)
                    scale = SCALE if j == 0 else 1.0
                    nc.scalar.activation(full[j][p][:], qk_ps[j][p][:], ACT.Identity,
                                         bias=bias_qk[:, j:j + 1], scale=scale).then_inc(act_done, 1)
                    nc.scalar.activation(parts[j][p][:, 0, :], qk_ps[j][p][:], ACT.Identity,
                                         bias=bias_qk[:, j:j + 1], scale=scale).then_inc(act_done, 1)
                for j in range(2):
                    wait(act, rest_done, b.n, 2, j + 1)
                    nc.scalar.copy(parts[j][p][:, 1, :], rest[j][p][:]).then_inc(act_done, 1)

            for b in BATCHES:
                step(b)

        @block.vector
        def _(dve):
            dve.sem_inc(v_copied, 1)

            def step(b):
                p = b.p
                for j in range(2):
                    wait(dve, act_done, b.n, 6, 12 + 2 * j + 2)
                    wait(dve, third_done, b.n, 2, 0)
                    nc.vector.tensor_tensor(rest[j][p][:], full[j][p][:], parts[j][p][:, 0, :],
                                            ALU.subtract).then_inc(rest_done, 1)
                wait(dve, v_ready, b.n, 1, 1)
                nc.vector.tensor_copy(v_all[:, b.n * QT:(b.n + 1) * QT, :],
                                      v_ps[p][:].rearrange("p (t c) -> p t c", c=C)).then_inc(v_copied, 1)
                for j in range(2):
                    wait(dve, act_done, b.n, 6, 12 + 5 + j)
                    nc.vector.tensor_tensor(parts[j][p][:, 2, :], rest[j][p][:], parts[j][p][:, 1, :],
                                            ALU.subtract).then_inc(third_done, 1)

            for b in BATCHES:
                step(b)


def attention(nc, x, w_proj, b_proj, q_parts, k_parts, ident, ident16, mask_q, mask_k, ones, v_all, x1):
    with ExitStack() as ctx:
        def sb(name, shape, dt=F32):
            return ctx.enter_context(nc.sbuf_tensor(name, shape, dt))

        def ps(name, shape):
            return ctx.enter_context(nc.psum_tensor(name, shape, F32))

        def sem(name):
            return ctx.enter_context(nc.semaphore(name))

        q_st = [sb(f"q_st{i}", [KTAU, H * T], BF16) for i in range(2)]
        k_st = [sb(f"k_st{i}", [P, H * T], BF16) for i in range(2)]
        v_pad = sb("v_pad", [P, QT, H, 32])
        w_sb = sb("wp_sb", [P, C])
        bp_sb = sb("bp_sb", [1, C])
        p_t = [sb(f"p_t{i}", [P, 4, 1280]) for i in range(2)]
        top = sb("top", [P, ROWSETS, CH, TOP])
        m_a = sb("m_a", [P, ROWSETS * CH * TOP])
        m_b = sb("m_b", [P, ROWSETS * CH * TOP])
        restart = sb("restart", [P, ROWSETS, 2 * TOP])
        recip_k = sb("recip_k", [P, ROWSETS, 2 * TOP])
        tau = sb("tau", [P, ROWSETS])
        neg_tau = sb("neg_tau", [P, ROWSETS])
        last_kept = sb("last_kept", [P, ROWSETS])
        short = sb("short", [P, ROWSETS], BF16)
        ones_col = sb("ones_col", [P, 1], BF16)
        short_any = sb("short_any", [1, ROWSETS])
        from_end = sb("from_end", [1, ROWSETS])
        countdown = sb("countdown", [1, ROWSETS])
        first_few = sb("first_few", [1, TOP])
        plan_i = sb("plan_i", [1, 2], I32)
        total = sb("total", [1, 1])
        list_i = sb("list_i", [1, TOP], I32)
        short_i = sb("short_i", [1, ROWSETS], I32)
        fix_tau = sb("fix_tau", [P, 1])
        fix_sum = sb("fix_sum", [P, 2])
        fix_over = sb("fix_over", [P, T], BF16)
        fix_open = sb("fix_open", [P, 1], BF16)
        open_i = sb("open_i", [1, 1], I32)
        zeros = sb("zeros", [P, T], BF16)
        fix_over2 = sb("fix_over2", [P, T], BF16)
        tau_t = sb("tau_t", [ROWSETS, P])
        tau_rest = sb("tau_rest", [ROWSETS, P])
        tau_parts = sb("tau_parts", [ROWSETS, PARTS, P], BF16)
        y_sb = sb("y_sb", [P, T])
        x_res = [sb(f"x_res{i}", [P, QT, C]) for i in range(2)]
        summed = sb("summed", [P, QT, C])
        stats = sb("stats", [P, QT, 6])
        moments = sb("moments", [P, QT, 2])
        rstd = sb("rstd", [P, QT])
        shifted = sb("shifted", [P, QT])
        minus_half = sb("minus_half", [P, QT])

        s_ps = [ps(f"s_ps{i}", [P, T]) for i in range(SBANKS)]
        t_ps = [ps(f"t_ps{i}", [P, T]) for i in range(2)]
        y_ps = ps("y_ps", [P, T])
        misc = ps("misc", [P, T])

        consts = sem("a_consts")
        loads = sem("a_loads")
        stacks = [sem(f"stacks{i}") for i in range(2)]
        x_in = [sem(f"x_in_sem{i}") for i in range(2)]
        tau_rows = [sem(f"tau_rows{i}") for i in range(2)]
        s_ready = sem("s_ready")
        s_free = sem("s_free")
        sort_step = sem("sort_step")
        tau_ready = sem("tau_ready")
        short_counted = sem("short_counted")
        flag_step = sem("flag_step")
        flags_ready = sem("flags_ready")
        fix_scores = sem("fix_scores")
        fix_done = sem("fix_done")
        fix_tried = sem("fix_tried")
        fix_counted = sem("fix_counted")
        tau_final = sem("tau_final")
        tau_turned = sem("tau_turned")
        tau_act = sem("tau_act")
        tau_pool = sem("tau_pool")
        t_ready = sem("t_ready")
        p_ready = sem("p_ready")
        av_done = sem("av_done")
        v_padded = sem("v_padded")
        y_copied = sem("y_copied")
        proj_ready = sem("proj_ready")
        proj_read = sem("proj_read")
        norm_step = sem("norm_step")
        var_shifted = sem("var_shifted")
        rstd_ready = sem("rstd_ready")
        x1_ready = sem("x1_ready")
        block = ctx.enter_context(nc.Block())

        SORT = 13
        NORM = 2

        def pipeline(first, step):
            first(BATCHES[0])
            for b, c in zip(BATCHES, BATCHES[1:] + [None]):
                step(b, c)

        def flagged_tiles(eng, body):
            listed = eng.value_load(plan_i[0:1, 0:1], min_val=0, max_val=TOP)
            with eng.If(listed):
                with eng.Fori(0, listed) as i:
                    body(eng.value_load(list_i[0:1, bass.ds(i, 1)], min_val=0, max_val=ROWSETS - 1))
                more = eng.value_load(plan_i[0:1, 1:2], min_val=0, max_val=1)
                with eng.If(more):
                    with eng.Fori(0, ROWSETS) as r:
                        flag = eng.value_load(short_i[0:1, bass.ds(r, 1)], min_val=0, max_val=1)
                        with eng.If(flag):
                            body(r)

        def take_turn(eng, sem):
            eng.wait_ge(sem, 1)
            eng.sem_clear(sem)

        @block.sync
        def _(sp):
            sp.dma_start(w_sb[:], w_proj).then_inc(loads, 16)
            sp.dma_start(bp_sb[:], b_proj.rearrange("(a n) -> a n", a=1)).then_inc(loads, 16)
            sp.wait_ge(consts, 2)

            def load(b):
                p = b.p
                base = b.n * (PARTS * C * T)
                for u in range(PARTS):
                    src = bass.AP(q_parts.tensor, base + u * C * T, [[0, PARTS], [H * T, HD], [1, H * T]])
                    sp.dma_start(q_st[p][24 * u:24 * u + 24, :], src).then_inc(stacks[p], 16)
                src = bass.AP(k_parts.tensor, base, [[0, PARTS], [H * T, PARTS * HD], [1, H * T]])
                sp.dma_start(k_st[p][0:KROWS, :], src).then_inc(stacks[p], 16)
                sp.dma_start(x_res[p][:], x[b.n].rearrange("(t p) c -> p t c", p=P)
                             ).then_inc(x_in[p], 16)

            load(BATCHES[0])
            load(BATCHES[1])

            def first(b):
                pass

            def step(b, c):
                wait(sp, tau_pool, b.n, 2, 2)
                for i in range(PARTS):
                    sp.dma_start(q_st[b.p][KROWS + i:KROWS + i + 1, :].rearrange("a (r t) -> a r t", t=P),
                                 tau_parts[:, i, :]).then_inc(tau_rows[b.p], 16)
                if b.n + 2 >= B:
                    return
                wait(sp, av_done, b.n, 4, 2 + 4)
                wait(sp, proj_read, b.n, 1, 1 + 1)
                load(BATCHES[b.n + 2])

            pipeline(first, step)

        @block.gpsimd
        def _(pool):
            for i in range(2):
                nc.gpsimd.memset(k_st[i][64:96, :], 1.0).then_inc(consts, 1)
                pool.wait_ge(consts, i + 1)
            nc.gpsimd.memset(v_pad[:], 0.0).then_inc(consts, 1)
            nc.gpsimd.memset(restart[:], 1.0).then_inc(consts, 1)
            nc.gpsimd.memset(minus_half[:], -0.5).then_inc(consts, 1)
            nc.gpsimd.memset(ones_col[:], 1.0).then_inc(consts, 1)
            for k in range(2 * TOP):
                nc.gpsimd.memset(recip_k[:, :, k:k + 1], 1.0 / (k + 1)).then_inc(consts, 1)
            nc.gpsimd.memset(zeros[:], 0.0).then_inc(consts, 1)
            nc.gpsimd.iota(countdown[:], pattern=[[-1, ROWSETS]], base=ROWSETS, channel_multiplier=0,
                           allow_small_or_imprecise_dtypes=True).then_inc(consts, 1)
            pool.wait_ge(consts, 4)
            nc.gpsimd.memset(restart[:, :, 0:1], 0.0).then_inc(consts, 1)
            pool.sem_inc(y_copied, 1)

            def first(b):
                pass

            def step(b, c):
                wait(pool, av_done, b.n, 4, 2)
                for r in range(4):
                    dst = v_pad[:].rearrange("p k (j r) c -> p (k j) r c", r=4)[:, :, r, HD * r:HD * r + HD]
                    src = v_all[:, b.n * QT:(b.n + 1) * QT, :].rearrange(
                        "p k (j r d) -> p (k j) r d", r=4, d=HD)[:, :, r, :]
                    last = nc.gpsimd.tensor_copy(dst, src)
                last.then_inc(v_padded, 1)
                wait(pool, tau_act, b.n, 3, 2)
                nc.gpsimd.tensor_tensor(tau_rest[:], tau_t[:], tau_parts[:, 0, :], ALU.subtract).then_inc(tau_pool, 1)
                wait(pool, tau_act, b.n, 3, 3)
                nc.gpsimd.tensor_tensor(tau_parts[:, 2, :], tau_rest[:], tau_parts[:, 1, :],
                                        ALU.subtract).then_inc(tau_pool, 1)
                wait(pool, norm_step, b.n, NORM, NORM)
                nc.gpsimd.tensor_scalar(shifted[:], moments[:, :, 1], EPS, None, ALU.add).then_inc(var_shifted, 1)
                wait(pool, var_shifted, b.n, 1, 1)
                nc.gpsimd.tensor_tensor(rstd[:], shifted[:], minus_half[:], ALU.pow).then_inc(rstd_ready, 1)

            pipeline(first, step)

        def scores(b, r):
            p, h, qt = b.p, r // QT, r % QT
            bank = s_ps[r % SBANKS]
            w = (qt + 1) * P
            nc.tensor.matmul(bank[:, 0:w], q_st[p][0:KROWS, h * T + qt * P:h * T + qt * P + P],
                             k_st[p][0:KROWS, h * T:h * T + w], start=True, stop=False)
            return nc.tensor.matmul(bank[:, w - P:w], ident16[:], mask_q[:, T - P:T], start=False, stop=True)

        def jobs():
            for j in range(4):
                yield [(j, 0)]
                yield [(j, 1), (j, 3)]
                if j % 2:
                    yield [(j - 1, 2), (j, 2)]

        KCOL = {0: 0, 1: 512, 3: 896, 2: 1024}

        @block.tensor
        def _(pe):
            pe.wait_ge(consts, 25)
            pe.wait_ge(loads, 32)
            pe.sem_inc(av_done, 2)
            pe.sem_inc(s_free, SBANKS)
            pe.sem_inc(proj_read, 1)
            pe.sem_inc(p_ready, 2)
            pe.sem_inc(fix_done, 1)

            def some_scores(b, rows):
                for r in rows:
                    if r == 0:
                        wait(pe, stacks[b.p], b.pair, 64, 64)
                    wait(pe, s_free, b.n, ROWSETS, r + 1)
                    scores(b, r).then_inc(s_ready, 1)

            def times_v(b, g):
                wait(pe, p_ready, b.n, JOBS, 10 * (g + 1) + 2)
                if g == 0:
                    wait(pe, v_padded, b.n, 1, 1)
                    wait(pe, y_copied, b.n, 1, 1)
                for kt in range(QT):
                    w = T - kt * P
                    for j in range(4):
                        last = nc.tensor.matmul(y_ps[32 * j:32 * j + 32, kt * P:T], v_pad[:, kt, 4 * j + g, :],
                                                p_t[g % 2][:, j, KCOL[kt]:KCOL[kt] + w],
                                                start=(g == 0 and kt == 0), stop=(g == 3 and kt == QT - 1))
                last.then_inc(av_done, 1)

            def scores_to_fix(b, r):
                p = b.p
                take_turn(pe, fix_done)
                wait(pe, y_copied, b.n, 1, 1)
                nc.tensor.matmul(misc[:], q_st[p][0:KROWS, bass.ds(r * P, P)],
                                 k_st[p][0:KROWS, bass.ds(r // QT * T, T)], start=True, stop=False)
                nc.tensor.matmul(misc[:], ident16[:], mask_q[:, bass.ds((QT - 1 - r % QT) * P, T)],
                                 start=False, stop=True).then_inc(fix_scores, 1)
                take_turn(pe, fix_tried)
                nc.tensor.matmul(y_ps[0:1, 0:1], fix_open[:], ones_col[:], start=True, stop=True
                                 ).then_inc(fix_counted, 1)

            def first(b):
                some_scores(b, range(ROWSETS))

            def step(b, c):
                p = b.p
                todo = list(range(ROWSETS)) if c else []

                def take(n):
                    now = todo[:n]
                    del todo[:n]
                    if now:
                        some_scores(c, now)

                take(16)
                wait(pe, tau_ready, b.n, 1, 1)
                wait(pe, proj_read, b.n, 1, 1)
                nc.tensor.matmul(misc[0:1, 0:ROWSETS], ones_col[:], short[:], start=True, stop=True
                                 ).then_inc(short_counted, 1)
                take(SBANKS)
                wait(pe, flags_ready, b.n, 1, 1)
                flagged_tiles(pe, lambda r: scores_to_fix(b, r))
                wait(pe, tau_final, b.n, 1, 1)
                nc.tensor.transpose(misc[0:ROWSETS, 0:P], neg_tau[:], ident[:]).then_inc(tau_turned, 1)
                take(12)
                n = 0
                for g in range(4):
                    for k, parts in enumerate(jobs()):
                        if g == 0 and k == 0:
                            wait(pe, tau_rows[p], b.pair, 48, 48)
                        wait(pe, p_ready, b.n, JOBS, n + 1)
                        bank = t_ps[n % 2]
                        col = 0
                        for j, kt in parts:
                            h, w = 4 * j + g, T - kt * P
                            nc.tensor.matmul(bank[:, col:col + w], k_st[p][0:KTAU, h * T + kt * P:h * T + kt * P + P],
                                             q_st[p][0:KTAU, h * T + kt * P:h * T + T], start=True, stop=False)
                            last = nc.tensor.matmul(bank[:, col:col + P], ident16[:], mask_k[:], start=False, stop=True)
                            col += w
                        last.then_inc(t_ready, 1)
                        n += 1
                        take(1)
                    if g:
                        times_v(b, g - 1)
                take(ROWSETS)
                times_v(b, 3)
                wait(pe, y_copied, b.n, 1, 2)
                wait(pe, tau_act, b.n, 3, 2)
                nc.tensor.matmul(misc[:], ones[0:1, :], bp_sb[0:1, :].unsqueeze(1).broadcast_to([1, QT, C]),
                                 start=True, stop=False)
                for t in range(QT):
                    last = nc.tensor.matmul(misc[:, t * P:(t + 1) * P], y_sb[:, t * P:(t + 1) * P], w_sb[:],
                                            start=False, stop=t == QT - 1)
                last.then_inc(proj_ready, 1)

            pipeline(first, step)

        @block.scalar
        def _(act):
            act.wait_ge(consts, 25)

            def first(b):
                pass

            def step(b, c):
                wait(act, tau_turned, b.n, 1, 1)
                wait(act, tau_pool, b.n, 2, 0)
                nc.scalar.copy(tau_t[:], misc[0:ROWSETS, 0:P]).then_inc(tau_act, 1)
                if b.n:
                    wait(act, tau_rows[1 - b.p], BATCHES[b.n - 1].pair, 48, 48)
                nc.scalar.copy(tau_parts[:, 0, :], misc[0:ROWSETS, 0:P]).then_inc(tau_act, 1)
                wait(act, tau_pool, b.n, 2, 1)
                nc.scalar.copy(tau_parts[:, 1, :], tau_rest[:]).then_inc(tau_act, 1)
                n = 0
                for g in range(4):
                    wait(act, av_done, b.n, 4, g + 1)
                    for parts in jobs():
                        wait(act, t_ready, b.n, JOBS, n + 1)
                        bank = t_ps[n % 2]
                        j, kt = parts[0]
                        if kt == 2:
                            out, src = (p_t[g % 2][:, j:j + 2, KCOL[2]:KCOL[2] + 256],
                                        bank[:].rearrange("p (a n) -> p a n", a=2))
                        else:
                            out, src = p_t[g % 2][:, j, KCOL[kt]:KCOL[kt] + T], bank[:]
                        nc.scalar.activation(out, src, ACT.Relu).then_inc(p_ready, 1)
                        n += 1
                wait(act, av_done, b.n, 4, 2 + 4)
                wait(act, proj_ready, b.n, 1, 0)
                nc.scalar.copy(y_sb[:], y_ps[:]).then_inc(y_copied, 1)

            pipeline(first, step)

        @block.vector
        def _(dve):
            dve.wait_ge(consts, 25)

            def search(b, rows):
                for r in rows:
                    wait(dve, s_ready, b.n, ROWSETS, r + 1)
                    w = (r % QT + 1) * P
                    chunks = s_ps[r % SBANKS][:, 0:w].rearrange("p (n c) -> p c n", c=CH)
                    for k in range(CH):
                        last = nc.vector.max(top[:, r, k, :], chunks[:, k, :])
                    last.then_inc(s_free, 1)

            def thresholds(b):
                n = [0]

                def link(ins):
                    n[0] += 1
                    ins.then_inc(sort_step, 1)
                    wait(dve, sort_step, b.n, SORT, n[0])

                wait(dve, s_free, b.n, ROWSETS, SBANKS + ROWSETS)

                def exchange(dst, src, size, stride, count):
                    s = src[:, 0:count].rearrange("p (g a s) -> p g a s", a=2, s=stride)
                    d = dst[:, 0:count].rearrange("p (g a s) -> p g a s", a=2, s=stride)
                    nc.vector.tensor_tensor(d[:, :, 0, :], s[:, :, 0, :], s[:, :, 1, :], ALU.max)
                    link(nc.vector.tensor_tensor(d[:, :, 1, :], s[:, :, 0, :], s[:, :, 1, :], ALU.min))

                pairs = top[:].rearrange("p r (m a) i -> p (r m) a i", a=2)
                merged = m_a[:].rearrange("p (g a i) -> p g a i", a=2, i=TOP)
                nc.vector.tensor_tensor(merged[:, :, 0, :], pairs[:, :, 0, :], pairs[:, :, 1, ::-1], ALU.max)
                link(nc.vector.tensor_tensor(merged[:, :, 1, :], pairs[:, :, 0, :], pairs[:, :, 1, ::-1], ALU.min))
                exchange(m_b, m_a, TOP, 4, ROWSETS * CH * TOP)
                exchange(m_a, m_b, TOP, 2, ROWSETS * CH * TOP)
                exchange(m_b, m_a, TOP, 1, ROWSETS * CH * TOP)
                two = m_b[:].rearrange("p (r m i) -> p r m i", m=2, i=2 * TOP)
                kept = ROWSETS * 2 * TOP
                link(nc.vector.tensor_tensor(m_a[:, 0:kept].rearrange("p (r i) -> p r i", i=2 * TOP),
                                             two[:, :, 0, :], two[:, :, 1, ::-1], ALU.max))
                exchange(m_b, m_a, 2 * TOP, 8, kept)
                exchange(m_a, m_b, 2 * TOP, 4, kept)
                exchange(m_b, m_a, 2 * TOP, 2, kept)
                exchange(m_a, m_b, 2 * TOP, 1, kept)
                ranked = m_a[:, 0:kept]
                prefix = m_b[:, 0:kept]
                link(nc.vector.tensor_tensor_scan(prefix, restart[:].rearrange("p r i -> p (r i)"), ranked, 0.0,
                                                  ALU.mult, ALU.add))
                link(nc.vector.scalar_tensor_tensor(out=prefix, in0=prefix, scalar=1.0,
                                                    in1=recip_k[:].rearrange("p r i -> p (r i)"),
                                                    op0=ALU.subtract, op1=ALU.mult))
                nc.vector.tensor_reduce(tau[:], prefix.rearrange("p (r i) -> p r i", i=2 * TOP), AX, ALU.max)
                link(nc.vector.tensor_reduce(last_kept[:], top[:, :, :, TOP - 1], AX, ALU.max))
                link(nc.vector.tensor_tensor(last_kept[:], last_kept[:],
                                             ranked.rearrange("p (r i) -> p r i", i=2 * TOP)[:, :, 2 * TOP - 1],
                                             ALU.max))
                nc.vector.tensor_tensor(short[:], last_kept[:], tau[:], ALU.is_gt).then_inc(tau_ready, 1)
                assert n[0] == SORT

            def flags(b):
                n = [0]

                def link(ins):
                    n[0] += 1
                    ins.then_inc(flag_step, 1)
                    wait(dve, flag_step, b.n, 3, n[0])

                wait(dve, short_counted, b.n, 1, 1)
                wait(dve, tau_ready, b.n, 1, 1)
                link(nc.vector.tensor_scalar(short_any[:], misc[0:1, 0:ROWSETS], 0.5, None, ALU.is_gt))
                nc.vector.tensor_copy(short_i[:], short_any[:])
                nc.vector.tensor_tensor(from_end[:], short_any[:], countdown[:], ALU.mult)
                link(nc.vector.tensor_reduce(total[:], short_any[:], AX, ALU.add))
                nc.vector.tensor_scalar(plan_i[0:1, 0:1], total[:], float(TOP), None, ALU.min)
                nc.vector.tensor_scalar(plan_i[0:1, 1:2], total[:], float(TOP), None, ALU.is_gt)
                link(nc.vector.max(first_few[:], from_end[:]))
                nc.vector.tensor_scalar(list_i[:], first_few[:], -1.0, float(ROWSETS), ALU.mult, ALU.add
                                        ).then_inc(flags_ready, 1)
                wait(dve, flags_ready, b.n, 1, 1)

            def newton_step():
                nc.vector.scalar_tensor_tensor(out=fix_over[:], in0=misc[:], scalar=fix_tau[:, 0:1], in1=zeros[:],
                                               op0=ALU.subtract, op1=ALU.max, accum_out=fix_sum[:, 0:1])
                nc.vector.tensor_scalar(fix_over2[:], misc[:], fix_tau[:, 0:1], 0.0,
                                        ALU.is_gt, ALU.add, accum_out=fix_sum[:, 1:2])
                dve.drain()
                nc.vector.reciprocal(fix_sum[:, 1:2], fix_sum[:, 1:2])
                nc.vector.tensor_scalar(fix_sum[:, 0:1], fix_sum[:, 0:1], 1.0, None, ALU.subtract)
                dve.drain()
                nc.vector.scalar_tensor_tensor(out=fix_tau[:], in0=fix_sum[:, 0:1], scalar=fix_sum[:, 1:2],
                                               in1=fix_tau[:], op0=ALU.mult, op1=ALU.add)
                dve.drain()

            def fix(r):
                nc.vector.tensor_copy(fix_tau[:], tau[:, bass.ds(r, 1)])
                take_turn(dve, fix_scores)
                dve.drain()
                with dve.Fori(0, FEW):
                    newton_step()
                nc.vector.tensor_scalar(fix_open[:], fix_sum[:, 0:1], CLOSE, None, ALU.is_gt
                                        ).then_inc(fix_tried, 1)
                take_turn(dve, fix_counted)
                nc.vector.tensor_copy(open_i[:], y_ps[0:1, 0:1])
                dve.drain()
                still = dve.value_load(open_i[0:1, 0:1], min_val=0, max_val=P)
                with dve.If(still):
                    with dve.Fori(0, NEWTON - FEW):
                        newton_step()
                nc.vector.tensor_copy(tau[:, bass.ds(r, 1)], fix_tau[:]).then_inc(fix_done, 1)
                dve.drain()

            def fix_thresholds(b):
                flagged_tiles(dve, fix)
                nc.vector.tensor_scalar(neg_tau[:], tau[:], -1.0, None, ALU.mult).then_inc(tau_final, 1)

            def normalise(b):
                n = [0]

                def link(ins):
                    n[0] += 1
                    ins.then_inc(norm_step, 1)
                    wait(dve, norm_step, b.n, NORM, n[0])

                wait(dve, proj_ready, b.n, 1, 1)
                wait(dve, x_in[b.p], b.pair, 16, 16)
                nc.vector.tensor_tensor(summed[:], misc[:].rearrange("p (t c) -> p t c", c=C), x_res[b.p][:],
                                        ALU.add).then_inc(proj_read, 1)
                wait(dve, proj_read, b.n, 1, 1 + 1)
                for t in range(QT):
                    last = nc.vector.bn_stats(stats[:, t, :], summed[:, t, :])
                link(last)
                for t in range(QT):
                    last = nc.vector.bn_aggr(moments[:, t, :], stats[:, t, :])
                link(last)
                wait(dve, rstd_ready, b.n, 1, 1)
                for t in range(QT):
                    last = nc.vector.tensor_scalar(x1[:, b.n * QT + t:b.n * QT + t + 1, :], summed[:, t:t + 1, :],
                                                   moments[:, t, 0:1], rstd[:, t:t + 1], ALU.subtract, ALU.mult)
                last.then_inc(x1_ready, 1)
                wait(dve, x1_ready, b.n, 1, 1)

            def first(b):
                search(b, range(ROWSETS))
                thresholds(b)

            def step(b, c):
                if c:
                    search(c, range(16))
                flags(b)
                fix_thresholds(b)
                if c:
                    search(c, range(16, ROWSETS))
                    thresholds(c)
                normalise(b)

            pipeline(first, step)


def router(nc, router_w, expert_bias, ident, x1, x1_t, gates_out):
    with ExitStack() as ctx:
        def sb(name, shape, dt=F32):
            return ctx.enter_context(nc.sbuf_tensor(name, shape, dt))

        def sem(name):
            return ctx.enter_context(nc.semaphore(name))

        rw = sb("rw", [P, NE])
        bias = sb("bias", [P, NE])
        order = sb("order", [P, NE])
        score = sb("score", [P, NT, NE])
        biased = sb("biased", [P, NT, NE])
        equal = sb("equal", [P, NT, NE])
        chosen = [sb(f"chosen{k}", [P, NT, NE]) for k in range(2)]
        most = sb("most", [P, NT])
        gates = sb("gates", [P, NT, NE])
        g_t = sb("g_t", [P, 2, P])
        tr = [ctx.enter_context(nc.psum_tensor(f"r_tr{i}", [P, T], F32)) for i in range(2)]
        lg = ctx.enter_context(nc.psum_tensor("lg", [P, T], F32))
        gt_ps = ctx.enter_context(nc.psum_tensor("gt_ps", [P, T], F32))
        loaded = sem("r_loaded")
        turned = sem("r_turned")
        copied = sem("r_copied")
        logits = sem("r_logits")
        ordered = sem("r_ordered")
        dstep = sem("r_step")
        exped = sem("r_exp")
        gates_done = sem("r_gates")
        g_turned = sem("r_g_turned")
        g_copied = sem("r_g_copied")
        g_stored = sem("r_g_stored")
        block = ctx.enter_context(nc.Block())

        @block.sync
        def _(sp):
            sp.dma_start(rw[:], router_w).then_inc(loaded, 16)
            sp.dma_start(bias[:], expert_bias.partition_broadcast(P)).then_inc(loaded, 16)
            sp.wait_ge(g_copied, 1)
            sp.dma_start(gates_out.rearrange("(a p) t -> p a t", p=P), g_t[:]).then_inc(g_stored, 16)
            sp.wait_ge(g_stored, 16)

        @block.tensor
        def _(pe):
            def turn(g):
                if g >= 2:
                    pe.wait_ge(copied, g - 1)
                for t in range(QT):
                    last = nc.tensor.transpose(tr[g % 2][:, t * P:(t + 1) * P], x1[:, g * QT + t, :], ident[:])
                last.then_inc(turned, 1)

            pe.wait_ge(loaded, 32)
            turn(0)
            for g in range(B):
                if g + 1 < B:
                    turn(g + 1)
                pe.wait_ge(copied, g + 1)
                for t in range(g * QT, (g + 1) * QT):
                    last = nc.tensor.matmul(lg[:, t * NE:(t + 1) * NE], x1_t[:, t * P:(t + 1) * P], rw[:],
                                            start=True, stop=True)
            last.then_inc(logits, 1)
            pe.wait_ge(gates_done, 1)
            for a in range(2):
                last = nc.tensor.transpose(gt_ps[:, a * P:(a + 1) * P],
                                           gates[:, a * (NT // 2):(a + 1) * (NT // 2), :].rearrange(
                                               "p t e -> p (t e)"), ident[:])
            last.then_inc(g_turned, 1)

        @block.gpsimd
        def _(pool):
            for e in range(NE):
                last = nc.gpsimd.memset(order[:, e:e + 1], float(NE - e))
            last.then_inc(ordered, 1)

        @block.scalar
        def _(act):
            for g in range(B):
                act.wait_ge(turned, g + 1)
                nc.scalar.copy(x1_t[:, g * T:(g + 1) * T], tr[g % 2][:]).then_inc(copied, 1)
            act.wait_ge(dstep, 2)
            nc.scalar.activation(score[:], score[:], ACT.Exp).then_inc(exped, 1)
            act.wait_ge(g_turned, 1)
            nc.scalar.copy(g_t[:].rearrange("p a t -> p (a t)"), gt_ps[:, 0:2 * P]).then_inc(g_copied, 1)

        @block.vector
        def _(dve):
            n = [0]

            def link(ins):
                n[0] += 1
                ins.then_inc(dstep, 1)
                dve.wait_ge(dstep, n[0])

            def over_experts(ap):
                return ap.unsqueeze(2).broadcast_to([P, NT, NE])

            lgv = lg[:, 0:NT * NE].rearrange("p (t e) -> p t e", e=NE)
            dve.wait_ge(logits, 1)
            dve.wait_ge(ordered, 1)
            dve.wait_ge(loaded, 32)
            link(nc.vector.tensor_reduce(most[:], lgv, AX, ALU.max))
            link(nc.vector.tensor_tensor(score[:], lgv, over_experts(most[:]), ALU.subtract))
            dve.wait_ge(exped, 1)
            link(nc.vector.tensor_reduce(most[:], score[:], AX, ALU.add))
            link(nc.vector.reciprocal(most[:], most[:]))
            link(nc.vector.tensor_tensor(score[:], score[:], over_experts(most[:]), ALU.mult))
            link(nc.vector.tensor_tensor(biased[:], score[:], bias[:].unsqueeze(1).broadcast_to([P, NT, NE]),
                                         ALU.add))
            for k in range(2):
                link(nc.vector.tensor_reduce(most[:], biased[:], AX, ALU.max))
                link(nc.vector.tensor_tensor(equal[:], biased[:], over_experts(most[:]), ALU.is_equal))
                link(nc.vector.tensor_tensor(equal[:], equal[:], order[:].unsqueeze(1).broadcast_to([P, NT, NE]),
                                             ALU.mult))
                link(nc.vector.tensor_reduce(most[:], equal[:], AX, ALU.max))
                link(nc.vector.tensor_tensor(chosen[k][:], equal[:], over_experts(most[:]), ALU.is_equal))
                if k == 0:
                    link(nc.vector.scalar_tensor_tensor(out=biased[:], in0=chosen[0][:], scalar=MASKED,
                                                        in1=biased[:], op0=ALU.mult, op1=ALU.add))
            link(nc.vector.tensor_tensor(gates[:], chosen[0][:], chosen[1][:], ALU.add))
            nc.vector.tensor_tensor(gates[:], gates[:], score[:], ALU.mult).then_inc(gates_done, 1)


def experts(nc, w1, w2, w3, sw1, sw2, sw3, ident, x1, x1_t, gates_in, out):
    with ExitStack() as ctx:
        def sb(name, shape, dt=F32):
            return ctx.enter_context(nc.sbuf_tensor(name, shape, dt))

        def ps(name):
            return ctx.enter_context(nc.psum_tensor(name, [P, T], F32))

        def sem(name):
            return ctx.enter_context(nc.semaphore(name))

        NJ = NE + 1
        wu = sb("wu", [P, NJ, C])
        wv = sb("wv", [P, NJ, C])
        wd = sb("wd", [P, NJ, C])
        gate = [sb(f"gate{i}", [P, QT, NE, P]) for i in range(2)]
        silu = [sb(f"silu{i}", [P, T]) for i in range(2)]
        hid = [sb(f"hid{i}", [P, T]) for i in range(2)]
        o_t = [sb(f"o_t{i}", [P, T]) for i in range(2)]
        summed = sb("f_summed", [P, QT, C])
        result = [sb(f"result{i}", [P, QT, C]) for i in range(2)]
        stats = sb("f_stats", [P, QT, 6])
        moments = sb("f_moments", [P, QT, 2])
        shifted = sb("f_shifted", [P, QT])
        rstd = sb("f_rstd", [P, QT])
        minus_half = sb("f_minus_half", [P, QT])
        a_ps = [ps(f"a_ps{i}") for i in range(2)]
        b_ps = [ps(f"b_ps{i}") for i in range(2)]
        o_ps = [ps(f"o_ps{i}") for i in range(2)]
        tr_ps = ps("tr_ps")

        w_loaded = sem("w_loaded")
        gate_loaded = [sem(f"gate_loaded{i}") for i in range(2)]
        half_set = sem("half_set")
        up_ready = sem("up_ready")
        silu_ready = sem("silu_ready")
        mult_step = sem("mult_step")
        hid_ready = sem("hid_ready")
        down_done = sem("down_done")
        o_copied = sem("o_copied")
        o_turned = sem("o_turned")
        o_read = sem("o_read")
        norm_step = sem("f_norm_step")
        var_shifted = sem("f_var_shifted")
        rstd_ready = sem("f_rstd_ready")
        scaled = sem("f_scaled")
        sent = [sem(f"sent{i}") for i in range(2)]
        block = ctx.enter_context(nc.Block())

        def pipeline(step):
            for b, before in zip(BATCHES + [None], [None] + BATCHES):
                step(b, before)

        @block.sync
        def _(sp):
            for dst, shared, routed in ((wu, sw1, w1), (wv, sw3, w3), (wd, sw2, w2)):
                sp.dma_start(dst[:, 0, :], shared).then_inc(w_loaded, 16)
                sp.dma_start(dst[:, 1:NJ, :], routed.rearrange("e p n -> p e n")).then_inc(w_loaded, 16)

            def load(b):
                src = bass.AP(gates_in.tensor, b.n * (QT * NE * P), [[0, P], [1, QT * NE * P]])
                sp.dma_start(gate[b.p][:].rearrange("p t e n -> p (t e n)"), src).then_inc(gate_loaded[b.p], 16)

            load(BATCHES[0])
            load(BATCHES[1])

            for b in BATCHES:
                if b.n + 2 < B:
                    wait(sp, hid_ready, b.n, NJ, NJ + 2)
                    load(BATCHES[b.n + 2])
                wait(sp, scaled, b.n, 1, 1)
                sp.dma_start(out[b.n].rearrange("(t p) c -> p t c", p=P), result[b.p][:]).then_inc(sent[b.p], 16)
            for p in range(2):
                sp.wait_ge(sent[p], 16 * (B // 2))

        @block.gpsimd
        def _(pool):
            nc.gpsimd.memset(minus_half[:], -0.5).then_inc(half_set, 1)
            pool.wait_ge(half_set, 1)

            def step(b, before):
                if before is None:
                    return
                wait(pool, norm_step, before.n, 2, 2)
                nc.gpsimd.tensor_scalar(shifted[:], moments[:, :, 1], EPS, None, ALU.add).then_inc(var_shifted, 1)
                wait(pool, var_shifted, before.n, 1, 1)
                nc.gpsimd.tensor_tensor(rstd[:], shifted[:], minus_half[:], ALU.pow).then_inc(rstd_ready, 1)

            pipeline(step)

        @block.tensor
        def _(pe):
            pe.wait_ge(w_loaded, 96)
            pe.sem_inc(hid_ready, 2)
            pe.sem_inc(down_done, 2)
            pe.sem_inc(o_copied, 2)
            pe.sem_inc(o_turned, 2)
            pe.sem_inc(o_read, 1)

            def up(b, k):
                s = (b.p * NJ + k) % 2
                wait(pe, hid_ready, b.n, NJ, k + 1)
                x_b = x1_t[:, b.n * T:(b.n + 1) * T]
                nc.tensor.matmul(a_ps[s][:], wu[:, k, :], x_b, start=True, stop=True)
                nc.tensor.matmul(b_ps[s][:], wv[:, k, :], x_b, start=True, stop=True).then_inc(up_ready, 1)

            def down(b, k):
                s = (b.p * NJ + k) % 2
                wait(pe, hid_ready, b.n, NJ, k + 3)
                if k == 0:
                    wait(pe, o_copied, b.n, 1, 1)
                nc.tensor.matmul(o_ps[b.p][:], wd[:, k, :], hid[s][:], start=k == 0, stop=k == NJ - 1
                                 ).then_inc(down_done, 1)

            def turn(b):
                wait(pe, o_copied, b.n, 1, 3)
                wait(pe, o_read, b.n, 1, 1)
                for t in range(QT):
                    last = nc.tensor.transpose(tr_ps[:, t * P:(t + 1) * P], o_t[b.p][:, t * P:(t + 1) * P], ident[:])
                last.then_inc(o_turned, 1)

            def step(b, before):
                if b is None:
                    down(before, NJ - 1)
                    turn(before)
                    return
                for k in range(NJ):
                    up(b, k)
                    if k:
                        down(b, k - 1)
                    elif before:
                        down(before, NJ - 1)
                    if k == 3 and before:
                        turn(before)

            pipeline(step)

        @block.scalar
        def _(act):
            def finish(b):
                wait(act, down_done, b.n, NJ, NJ + 2)
                wait(act, o_turned, b.n, 1, 1)
                nc.scalar.copy(o_t[b.p][:], o_ps[b.p][:]).then_inc(o_copied, 1)

            def step(b, before):
                if b is None:
                    finish(before)
                    return
                for k in range(NJ):
                    s = (b.p * NJ + k) % 2
                    wait(act, up_ready, b.n, NJ, k + 1)
                    nc.scalar.activation(silu[s][:], a_ps[s][:], ACT.Silu).then_inc(silu_ready, 1)
                    if k == 2 and before:
                        finish(before)

            pipeline(step)

        @block.vector
        def _(dve):
            def moments_of(b):
                wait(dve, o_turned, b.n, 1, 3)
                nc.vector.tensor_tensor(summed[:], tr_ps[:].rearrange("p (t c) -> p t c", c=C),
                                        x1[:, b.n * QT:(b.n + 1) * QT, :], ALU.add).then_inc(o_read, 1)
                wait(dve, o_read, b.n, 1, 2)
                for t in range(QT):
                    last = nc.vector.bn_stats(stats[:, t, :], summed[:, t, :])
                last.then_inc(norm_step, 1)
                wait(dve, norm_step, b.n, 2, 1)
                for t in range(QT):
                    last = nc.vector.bn_aggr(moments[:, t, :], stats[:, t, :])
                last.then_inc(norm_step, 1)

            def scale(b):
                wait(dve, rstd_ready, b.n, 1, 1)
                wait(dve, norm_step, b.n, 2, 2)
                wait(dve, sent[b.p], b.pair, 16, 0)
                for t in range(QT):
                    last = nc.vector.tensor_scalar(result[b.p][:, t, :], summed[:, t, :],
                                                   moments[:, t, 0:1], rstd[:, t:t + 1], ALU.subtract, ALU.mult)
                last.then_inc(scaled, 1)
                wait(dve, scaled, b.n, 1, 1)

            def step(b, before):
                if b is None:
                    moments_of(before)
                    scale(before)
                    return
                for k in range(NJ):
                    s = (b.p * NJ + k) % 2
                    wait(dve, silu_ready, b.n, NJ, k + 1)
                    wait(dve, down_done, b.n, NJ, k + 1)
                    product = nc.vector.tensor_tensor(hid[s][:], b_ps[s][:], silu[s][:], ALU.mult)
                    if k:
                        product.then_inc(mult_step, 1)
                        wait(dve, mult_step, b.n, NE, k)
                        if k == 1:
                            wait(dve, gate_loaded[b.p], b.pair, 16, 16)
                        h4 = hid[s][:].rearrange("p (t n) -> p t n", n=P)
                        product = nc.vector.tensor_tensor(h4, h4, gate[b.p][:, :, k - 1, :], ALU.mult)
                    product.then_inc(hid_ready, 1)
                    if k == 4 and before:
                        moments_of(before)
                    if k == 6 and before:
                        scale(before)

            pipeline(step)


def program(nc, x, w_attn, b_attn, w_proj, b_proj, router_w, expert_bias, w1, w2, w3, sw1, sw2, sw3, out):
    q_parts = nc.dram_tensor("q_parts", (B, PARTS, C, T), BF16).ap()
    k_parts = nc.dram_tensor("k_parts", (B, PARTS, C, T), BF16).ap()
    gates = nc.dram_tensor("gates_t", (NT * NE, P), F32).ap()
    with ExitStack() as ctx:
        def sb(name, shape, dt=F32):
            return ctx.enter_context(nc.sbuf_tensor(name, shape, dt))

        ident = sb("ident", [P, P])
        ident16 = sb("ident16", [P, P], BF16)
        mask_q = sb("mask_q", [P, 2 * T - P], BF16)
        mask_k = sb("mask_k", [P, P], BF16)
        ones = sb("ones", [1, P])
        x1 = sb("x1", [P, NT, C])
        with ExitStack() as inner:
            v_all = inner.enter_context(nc.sbuf_tensor("v_all", [P, NT, C], F32))
            setup_and_projections(nc, x, w_attn, b_attn, q_parts, k_parts, ident, ident16, mask_q, mask_k,
                                  ones, v_all)
            attention(nc, x, w_proj, b_proj, q_parts, k_parts, ident, ident16, mask_q, mask_k, ones, v_all, x1)
        x1_t = sb("x1_t", [P, B * T])
        router(nc, router_w, expert_bias, ident, x1, x1_t, gates)
        experts(nc, w1, w2, w3, sw1, sw2, sw3, ident, x1, x1_t, gates, out)


_INS = ["L0_attn_x", "L0_attn_w_attn", "L0_attn_b_attn", "L0_attn_w_proj", "L0_attn_b_proj",
        "L0_ffn_router_w", "L0_ffn_expert_bias", "L0_ffn_w1", "L0_ffn_w2", "L0_ffn_w3",
        "L0_ffn_sw1", "L0_ffn_sw2", "L0_ffn_sw3"]


def kernel(**inputs):
    import numpy as _np
    import concourse.bacc as _bacc
    from concourse import mybir as _mybir
    from concourse.bass_utils import run_bass_kernel_spmd as _run

    nc = _bacc.Bacc("TRN2", target_bir_lowering=False, num_devices=1)
    arrays, args = {}, []
    for name in _INS:
        a = _np.ascontiguousarray(inputs[name])
        arrays[f"in_{name}"] = a
        args.append(nc.dram_tensor(f"in_{name}", a.shape, _mybir.dt.from_np(a.dtype), kind="ExternalInput").ap())
    args.append(nc.dram_tensor("out_0", (B, T, C), _mybir.dt.float32, kind="ExternalOutput").ap())
    program(nc, *args)
    r = _run(nc, [arrays], core_ids=[0])
    return r.results[0]["out_0"]
```

```python
import concourse.bass as bass
from concourse import mybir
from contextlib import ExitStack

F32 = mybir.dt.float32
BF16 = mybir.dt.bfloat16
I32 = mybir.dt.int32
ALU = mybir.AluOpType
ACT = mybir.ActivationFunctionType
AX = mybir.AxisListType.X

B, T, C = 8, 512, 128
H = 16
HD = C // H
P = 128
QT = T // P
NT = B * QT
NE = 8
PARTS = 3
KROWS = PARTS * PARTS * HD
KTAU = KROWS + PARTS
ROWSETS = H * QT
CH = 4
TOP = 8
NJ = NE + 1
HALF = T // 2
TILES = 2 * NJ
LAG = 2
FIRST = 12
BEFORE = 3
NORM = 2
SORT = 13
ROUTE = 18
MASKED = -1e30
EPS = 1e-5
SBANKS = 3
NEWTON = 24
FEW = 3
CLOSE = 3e-6
JOBS = 40
SCALE = 1.0 / float(HD) ** 0.5


class Batch:

    def __init__(self, n):
        self.n, self.pair, self.p = n, n // 2, n % 2


BATCHES = [Batch(n) for n in range(B)]


def tiles_of_transposed(g):
    for j in range(4):
        yield 0, [(j, 0)]
    for j in range(4):
        yield 1, [(j, 1), (j, 3)]
    for j in (0, 2):
        yield 2, [(j, 2), (j + 1, 2)]


def schedule():
    def known(n):
        return BATCHES[n] if 0 <= n < B else None

    items = []

    def add(kind, b, *args):
        if b is not None:
            items.append((kind, b) + args)

    def project(b, between):
        for kind in (("project_x",), ("project_qk", 0), ("project_qk", 1), ("project_v",), ("second_parts",)):
            add(kind[0], b, *kind[1:])
            between()
        add("store_parts", b)

    project(BATCHES[0], lambda: None)
    add("load_stacks", BATCHES[0])
    for s in range(-1, B + 2):
        c, b, f, o, p = known(s + 1), known(s), known(s - 1), known(s - 2), known(s + 2)
        row = [0]
        ups = [0]

        def scores(n):
            for _ in range(n):
                if row[0] < ROWSETS:
                    add("scores", c, row[0])
                    row[0] += 1

        def experts(n):
            for _ in range(n):
                if ups[0] < TILES + LAG:
                    j = ups[0]
                    if j < TILES:
                        add("up", o, j)
                    if j >= LAG:
                        add("down", o, j - LAG)
                    ups[0] += 1

        add("load_residual", f)
        experts(FIRST)
        add("count_short", b)
        add("residual", f)
        add("flags", b)
        experts(2)
        add("fix", b)
        add("turn_tau", b)
        add("scale_x1", f)
        experts(3)
        scores(BEFORE)
        experts(TILES + LAG)
        add("pad_v", b)
        between = {1: [("copy_out", o), ("turn_out", o)], 3: [("sum_out", o)], 4: [("turn_x1", f)],
                   6: [("logits", f)], 8: [("softmax", f), ("scale_out", o)], 10: [("gates", f)],
                   14: [("turn_gates", f)]}
        if p:
            between.update({18: [("project_x", p)], 21: [("project_qk", p, 0)], 24: [("project_qk", p, 1)],
                            27: [("project_v", p)], 30: [("second_parts", p)], 31: [("store_parts", p)]})
        waiting = []
        n = 0
        for g in range(4):
            for block, parts in tiles_of_transposed(g):
                add("transposed", b, n, g, block, parts)
                if waiting and (n - waiting[0][2] >= 2):
                    gg, bb, _ = waiting.pop(0)
                    add("times_v", b, gg, bb)
                n += 1
                if n in (4, 8, 10, 14, 18, 20, 24, 28, 30, 34, 38, 40):
                    waiting.append((g, block, n))
                scores(2 if n % 2 else 1)
                for kind, who, *more in between.get(n, ()):
                    add(kind, who, *more)
        scores(ROWSETS)
        for gg, bb, _ in waiting:
            add("times_v", b, gg, bb)
        add("copy_y", b)
        add("project_y", b)
        add("sort", c)
        add("load_stacks", p)
    return items


def program(nc, x, w_attn, b_attn, w_proj, b_proj, router_w, expert_bias, w1, w2, w3, sw1, sw2, sw3, out):
    q_parts = nc.dram_tensor("q_parts", (B, PARTS, C, T), BF16).ap()
    k_parts = nc.dram_tensor("k_parts", (B, PARTS, C, T), BF16).ap()
    gates_dram = nc.dram_tensor("gates_t", (NT * NE, P), F32).ap()
    ctx = ExitStack()
    with ctx:
        def sb(name, shape, dt=F32):
            return ctx.enter_context(nc.sbuf_tensor(name, shape, dt))

        def ps(name):
            return ctx.enter_context(nc.psum_tensor(name, [P, T], F32))

        def sem(name):
            return ctx.enter_context(nc.semaphore(name))

        ident = sb("ident", [P, P])
        ident16 = sb("ident16", [P, P], BF16)
        mask_q = sb("mask_q", [P, 2 * T - P], BF16)
        mask_k = sb("mask_k", [P, P], BF16)
        ones = sb("ones", [1, P])
        ones_col = sb("ones_col", [P, 1], BF16)
        zeros = sb("zeros", [P, T], BF16)
        restart = sb("restart", [P, ROWSETS, 2 * TOP], BF16)
        recip_k = sb("recip_k", [P, 2 * TOP])
        countdown = sb("countdown", [1, ROWSETS])
        minus_half = sb("minus_half", [P, QT])
        order = sb("order", [P, NE])
        w_sb = sb("w_sb", [P, 3 * C])
        bias_qk = sb("bias_qk", [P, 2])
        bias_v = sb("bias_v", [1, C])
        wp_sb = sb("wp_sb", [P, C])
        bp_sb = sb("bp_sb", [1, C])
        rw = sb("rw", [P, NE])
        bias_e = sb("bias_e", [P, NE])
        wu = sb("wu", [P, NJ, C])
        wv = sb("wv", [P, NJ, C])
        wd = sb("wd", [P, NJ, C])
        x_in = sb("x_in", [P, QT, C])
        x_t = sb("x_t", [P, T])
        rest = [sb(f"rest{j}", [P, T]) for j in range(2)]
        parts = [sb(f"parts{j}", [P, PARTS, T], BF16) for j in range(2)]
        v_nat = [sb(f"v_nat{i}", [P, QT, C]) for i in range(3)]
        q_st = [sb(f"q_st{i}", [KTAU, H * T], BF16) for i in range(2)]
        k_st = [sb(f"k_st{i}", [P, H * T], BF16) for i in range(2)]
        v_pad = sb("v_pad", [P, QT, H, 32])
        p_t = [sb("p_t0", [P, 4, T]), sb("p_t1", [P, 4, T]), sb("p_t2", [P, 4, 2 * P])]
        top = sb("top", [P, ROWSETS, CH, TOP])
        m_a = sb("m_a", [P, ROWSETS * CH * TOP])
        m_b = sb("m_b", [P, ROWSETS * CH * TOP])
        tau = sb("tau", [P, ROWSETS])
        neg_tau = sb("neg_tau", [P, ROWSETS])
        last_kept = sb("last_kept", [P, ROWSETS])
        short = sb("short", [P, ROWSETS], BF16)
        short_any = sb("short_any", [1, ROWSETS])
        from_end = sb("from_end", [1, ROWSETS])
        first_few = sb("first_few", [1, TOP])
        total = sb("total", [1, 1])
        plan_i = sb("plan_i", [1, 2], I32)
        list_i = sb("list_i", [1, TOP], I32)
        short_i = sb("short_i", [1, ROWSETS], I32)
        fix_tau = sb("fix_tau", [P, 1])
        fix_sum = sb("fix_sum", [P, 2])
        fix_over = sb("fix_over", [P, T], BF16)
        fix_over2 = sb("fix_over2", [P, T], BF16)
        fix_open = sb("fix_open", [P, 1], BF16)
        open_i = sb("open_i", [1, 1], I32)
        tau_t = sb("tau_t", [ROWSETS, P])
        tau_rest = sb("tau_rest", [ROWSETS, P])
        tau_parts = sb("tau_parts", [ROWSETS, PARTS, P], BF16)
        y_sb = sb("y_sb", [P, T])
        x_res = sb("x_res", [P, QT, C])
        summed = sb("summed", [P, QT, C])
        stats = sb("stats", [P, QT, 6])
        moments = sb("moments", [P, QT, 2])
        shifted = sb("shifted", [P, QT])
        rstd = sb("rstd", [P, QT])
        x1 = [sb(f"x1_{i}", [P, QT, C]) for i in range(3)]
        x1_t = sb("x1_t", [P, T])
        score = sb("score", [P, QT, NE])
        biased = sb("biased", [P, QT, NE])
        equal = sb("equal", [P, QT, NE])
        chosen = [sb(f"chosen{k}", [P, QT, NE]) for k in range(2)]
        most = sb("most", [P, QT])
        gates = sb("gates", [P, QT, NE])
        g_t = sb("g_t", [QT * NE, P])
        gate = [sb(f"gate{i}", [P, QT // 2, NE, P]) for i in range(2)]
        silu = [sb(f"silu{i}", [P, HALF]) for i in range(2)]
        lin = [sb(f"lin{i}", [P, HALF]) for i in range(2)]
        hid = [sb(f"hid{i}", [P, HALF]) for i in range(LAG + 1)]
        o_t = sb("o_t", [P, T])
        f_summed = sb("f_summed", [P, QT, C])
        f_stats = sb("f_stats", [P, QT, 6])
        f_moments = sb("f_moments", [P, QT, 2])
        f_shifted = sb("f_shifted", [P, QT])
        f_rstd = sb("f_rstd", [P, QT])

        s_ps = [ps(f"s_ps{i}") for i in range(SBANKS)]
        t_ps = [ps(f"t_ps{i}") for i in range(2)]
        y_ps = ps("y_ps")
        misc = ps("misc")
        work = ps("work")
        o_ps = t_ps[1]

        consts = sem("consts")
        consts2 = sem("consts2")
        loaded = sem("loaded")
        x_loaded = sem("x_loaded")
        pre_ready = sem("pre_ready")
        pre_act = sem("pre_act")
        pre_pool = sem("pre_pool")
        stored = sem("stored")
        stacks = [sem(f"stacks{i}") for i in range(2)]
        tau_rows = sem("tau_rows")
        s_ready = sem("s_ready")
        s_free = sem("s_free")
        sort_step = sem("sort_step")
        tau_ready = sem("tau_ready")
        short_counted = sem("short_counted")
        flag_step = sem("flag_step")
        flags_ready = sem("flags_ready")
        fix_scores = sem("fix_scores")
        fix_tried = sem("fix_tried")
        fix_counted = sem("fix_counted")
        fix_done = sem("fix_done")
        tau_final = sem("tau_final")
        tau_turned = sem("tau_turned")
        tau_act = sem("tau_act")
        tau_pool = sem("tau_pool")
        t_ready = sem("t_ready")
        p_ready = sem("p_ready")
        av_done = sem("av_done")
        v_padded = sem("v_padded")
        y_copied = sem("y_copied")
        y_projected = sem("y_projected")
        res_loaded = sem("res_loaded")
        residual_read = sem("residual_read")
        norm_step = sem("norm_step")
        var_shifted = sem("var_shifted")
        rstd_ready = sem("rstd_ready")
        x1_ready = sem("x1_ready")
        x1_turned = sem("x1_turned")
        x1_copied = sem("x1_copied")
        logits_ready = sem("logits_ready")
        route_step = sem("route_step")
        exped = sem("exped")
        gates_ready = sem("gates_ready")
        gates_turned = sem("gates_turned")
        gates_copied = sem("gates_copied")
        gates_stored = sem("gates_stored")
        gate_loaded = [sem(f"gate_loaded{i}") for i in range(2)]
        up_ready = sem("up_ready")
        up_act = sem("up_act")
        gate_step = sem("gate_step")
        hid_ready = sem("hid_ready")
        down_done = sem("down_done")
        o_copied = sem("o_copied")
        o_turned = sem("o_turned")
        o_read = sem("o_read")
        f_norm_step = sem("f_norm_step")
        f_var_shifted = sem("f_var_shifted")
        f_rstd_ready = sem("f_rstd_ready")
        result_ready = sem("result_ready")
        sent = sem("sent")
        block = ctx.enter_context(nc.Block())

        items = schedule()
        CONSTS = 33

        def each(eng, parts_of):
            for kind, b, *args in items:
                if kind in parts_of:
                    parts_of[kind](b, *args)

        def flagged_tiles(eng, body):
            listed = eng.value_load(plan_i[0:1, 0:1], min_val=0, max_val=TOP)
            with eng.If(listed):
                with eng.Fori(0, listed) as i:
                    body(eng.value_load(list_i[0:1, bass.ds(i, 1)], min_val=0, max_val=ROWSETS - 1))
                more = eng.value_load(plan_i[0:1, 1:2], min_val=0, max_val=1)
                with eng.If(more):
                    with eng.Fori(0, ROWSETS) as r:
                        flag = eng.value_load(short_i[0:1, bass.ds(r, 1)], min_val=0, max_val=1)
                        with eng.If(flag):
                            body(r)

        def take_turn(eng, sem):
            eng.wait_ge(sem, 1)
            eng.sem_clear(sem)

        @block.sync
        def _(sp):
            def load_x(b):
                sp.dma_start(x_in[:], x[b.n].rearrange("(t p) c -> p t c", p=P)).then_inc(x_loaded, 16)

            load_x(BATCHES[0])
            sp.dma_start(w_sb[:], w_attn).then_inc(loaded, 16)
            sp.dma_start(bias_qk[:], b_attn[0:2 * C].rearrange("(j p) -> p j", p=P),
                         allow_slow_non_contiguous=True).then_inc(loaded, 16)
            sp.dma_start(bias_v[:], b_attn[2 * C:3 * C].rearrange("(a n) -> a n", a=1)).then_inc(loaded, 16)
            sp.dma_start(wp_sb[:], w_proj).then_inc(loaded, 16)
            sp.dma_start(bp_sb[:], b_proj.rearrange("(a n) -> a n", a=1)).then_inc(loaded, 16)
            sp.dma_start(rw[:], router_w).then_inc(loaded, 16)
            sp.dma_start(bias_e[:], expert_bias.partition_broadcast(P)).then_inc(loaded, 16)
            for dst, shared, routed in ((wu, sw1, w1), (wv, sw3, w3), (wd, sw2, w2)):
                sp.dma_start(dst[:, 0, :], shared).then_inc(loaded, 16)
                sp.dma_start(dst[:, 1:NJ, :], routed.rearrange("e p n -> p e n")).then_inc(loaded, 16)

            def project_x(b):
                if b.n + 1 < B:
                    sp.wait_ge(pre_ready, 4 * b.n + 1)
                    load_x(BATCHES[b.n + 1])

            def store_parts(b):
                sp.wait_ge(pre_pool, 4 * b.n + 4)
                for j, dst in enumerate((q_parts, k_parts)):
                    for i in range(PARTS):
                        to = bass.AP(dst.tensor, (b.n * PARTS + i) * (C * T), [[T, H], [H * T, HD], [1, T]])
                        sp.dma_start(to, parts[j][:, i, :]).then_inc(stored, 16)

            def load_stacks(b):
                sp.wait_ge(stored, 96 * b.n + 96)
                if b.n < 2:
                    sp.wait_ge(consts, 2)
                else:
                    sp.wait_ge(av_done, 12 * (b.n - 2) + 12)
                p = b.p
                base = b.n * (PARTS * C * T)
                for u in range(PARTS):
                    src = bass.AP(q_parts.tensor, base + u * C * T, [[0, PARTS], [H * T, HD], [1, H * T]])
                    sp.dma_start(q_st[p][24 * u:24 * u + 24, :], src).then_inc(stacks[p], 16)
                src = bass.AP(k_parts.tensor, base, [[0, PARTS], [H * T, PARTS * HD], [1, H * T]])
                sp.dma_start(k_st[p][0:KROWS, :], src).then_inc(stacks[p], 16)

            def turn_tau(b):
                sp.wait_ge(tau_pool, 2 * b.n + 2)
                for i in range(PARTS):
                    sp.dma_start(q_st[b.p][KROWS + i:KROWS + i + 1, :].rearrange("a (r t) -> a r t", t=P),
                                 tau_parts[:, i, :]).then_inc(tau_rows, 16)

            def load_residual(b):
                sp.wait_ge(residual_read, b.n)
                sp.dma_start(x_res[:], x[b.n].rearrange("(t p) c -> p t c", p=P)).then_inc(res_loaded, 16)

            def turn_gates(b):
                sp.wait_ge(gates_copied, b.n + 1)
                rows = QT * NE
                sp.dma_start(gates_dram[b.n * rows:(b.n + 1) * rows, :], g_t[:]).then_inc(gates_stored, 16)
                sp.wait_ge(gates_stored, 16 * b.n + 16)
                sp.wait_ge(hid_ready, TILES * b.n)
                for i in range(2):
                    size = rows // 2 * P
                    src = bass.AP(gates_dram.tensor, (2 * b.n + i) * size, [[0, P], [1, size]])
                    sp.dma_start(gate[i][:].rearrange("p t e n -> p (t e n)"), src).then_inc(gate_loaded[i], 16)

            def scale_out(b):
                sp.wait_ge(result_ready, b.n + 1)
                sp.dma_start(out[b.n].rearrange("(t p) c -> p t c", p=P), f_summed[:]).then_inc(sent, 16)

            each(sp, dict(project_x=project_x, store_parts=store_parts, load_stacks=load_stacks,
                          turn_tau=turn_tau, load_residual=load_residual, turn_gates=turn_gates,
                          scale_out=scale_out))
            sp.wait_ge(sent, 16 * B)

        @block.gpsimd
        def _(pool):
            for i in range(2):
                nc.gpsimd.memset(k_st[i][64:96, :], 1.0).then_inc(consts, 1)
                pool.wait_ge(consts, i + 1)
            nc.gpsimd.memset(ident[:], 0.0).then_inc(consts, 1)
            nc.gpsimd.memset(mask_q[:], 0.0).then_inc(consts, 1)
            nc.gpsimd.memset(mask_k[:], 0.0).then_inc(consts, 1)
            nc.gpsimd.memset(ones[:], 1.0).then_inc(consts, 1)
            nc.gpsimd.memset(restart[:], 1.0).then_inc(consts, 1)
            pool.wait_ge(consts, 7)
            nc.gpsimd.affine_select(out=ident[:], in_=ident[:], compare_op=ALU.not_equal, fill=1.0,
                                    base=0, pattern=[[-1, P]], channel_multiplier=1).then_inc(consts, 1)
            nc.gpsimd.affine_select(out=mask_q[:], in_=mask_q[:], compare_op=ALU.is_ge, fill=MASKED,
                                    base=T - P, pattern=[[-1, 2 * T - P]],
                                    channel_multiplier=1).then_inc(consts, 1)
            nc.gpsimd.affine_select(out=mask_k[:], in_=mask_k[:], compare_op=ALU.is_ge, fill=MASKED,
                                    base=0, pattern=[[1, P]], channel_multiplier=-1).then_inc(consts, 1)
            nc.gpsimd.memset(restart[:, :, 0:1], 0.0).then_inc(consts, 1)
            pool.wait_ge(consts, 11)
            nc.gpsimd.tensor_copy(ident16[:], ident[:]).then_inc(consts, 1)
            nc.gpsimd.memset(v_pad[:], 0.0).then_inc(consts, 1)
            nc.gpsimd.memset(minus_half[:], -0.5).then_inc(consts, 1)
            nc.gpsimd.memset(ones_col[:], 1.0).then_inc(consts, 1)
            nc.gpsimd.memset(zeros[:], 0.0).then_inc(consts, 1)
            nc.gpsimd.iota(countdown[:], pattern=[[-1, ROWSETS]], base=ROWSETS, channel_multiplier=0,
                           allow_small_or_imprecise_dtypes=True).then_inc(consts, 1)
            for k in range(2 * TOP):
                last = nc.gpsimd.memset(recip_k[:, k:k + 1], 1.0 / (k + 1))
                last.then_inc(consts, 1)
            for e in range(NE):
                last = nc.gpsimd.memset(order[:, e:e + 1], float(NE - e))
            last.then_inc(consts2, 1)
            pool.wait_ge(consts2, 1)

            def project_qk(b, j):
                pool.wait_ge(pre_act, 8 * b.n + 3 + 2 * j)
                nc.gpsimd.tensor_tensor(rest[j][:], rest[j][:], parts[j][:, 0, :], ALU.subtract
                                        ).then_inc(pre_pool, 1)

            def second_parts(b):
                for j in range(2):
                    pool.wait_ge(pre_act, 8 * b.n + 7 + j)
                    nc.gpsimd.tensor_tensor(parts[j][:, 2, :], rest[j][:], parts[j][:, 1, :], ALU.subtract
                                            ).then_inc(pre_pool, 1)

            def turn_tau(b):
                pool.wait_ge(tau_act, 3 * b.n + 2)
                nc.gpsimd.tensor_tensor(tau_rest[:], tau_t[:], tau_parts[:, 0, :], ALU.subtract).then_inc(tau_pool, 1)
                pool.wait_ge(tau_act, 3 * b.n + 3)
                nc.gpsimd.tensor_tensor(tau_parts[:, 2, :], tau_rest[:], tau_parts[:, 1, :],
                                        ALU.subtract).then_inc(tau_pool, 1)

            def pad_v(b):
                pool.wait_ge(av_done, 12 * b.n)
                pool.wait_ge(pre_act, 8 * b.n + 6)
                for r in range(4):
                    dst = v_pad[:].rearrange("p k (j r) c -> p (k j) r c", r=4)[:, :, r, HD * r:HD * r + HD]
                    src = v_nat[b.n % 3][:].rearrange("p k (j r d) -> p (k j) r d", r=4, d=HD)[:, :, r, :]
                    last = nc.gpsimd.tensor_copy(dst, src)
                last.then_inc(v_padded, 1)

            def one_over_deviation(b, step, moments, shifted, var_shifted, rstd, ready):
                pool.wait_ge(step, NORM * b.n + NORM)
                nc.gpsimd.tensor_scalar(shifted[:], moments[:, :, 1], EPS, None, ALU.add).then_inc(var_shifted, 1)
                pool.wait_ge(var_shifted, b.n + 1)
                nc.gpsimd.tensor_tensor(rstd[:], shifted[:], minus_half[:], ALU.pow).then_inc(ready, 1)

            def residual(b):
                one_over_deviation(b, norm_step, moments, shifted, var_shifted, rstd, rstd_ready)

            def sum_out(b):
                one_over_deviation(b, f_norm_step, f_moments, f_shifted, f_var_shifted, f_rstd, f_rstd_ready)

            def up(b, j):
                half, k, h = j // NJ, j % NJ, hid[j % (LAG + 1)]
                pool.wait_ge(up_act, 2 * TILES * b.n + 2 * j + 2)
                if b.n or j > LAG:
                    pool.wait_ge(down_done, TILES * b.n + j - LAG)
                product = nc.gpsimd.tensor_tensor(h[:], silu[j % 2][:], lin[j % 2][:], ALU.mult)
                if k:
                    product.then_inc(gate_step, 1)
                    pool.wait_ge(gate_step, 2 * NE * b.n + half * NE + k)
                    if k == 1:
                        pool.wait_ge(gate_loaded[half], 16 * b.n + 16)
                    h3 = h[:].rearrange("p (t n) -> p t n", n=P)
                    product = nc.gpsimd.tensor_tensor(h3, h3, gate[half][:, :, k - 1, :], ALU.mult)
                product.then_inc(hid_ready, 1)

            each(pool, dict(project_qk=project_qk, second_parts=second_parts, turn_tau=turn_tau,
                            pad_v=pad_v, residual=residual, sum_out=sum_out, up=up))

        @block.tensor
        def _(pe):
            pe.wait_ge(consts, CONSTS)
            pe.wait_ge(loaded, 16 * 13)
            pe.sem_inc(s_free, SBANKS)
            pe.sem_inc(fix_done, 1)

            def project_x(b):
                pe.wait_ge(x_loaded, 16 * b.n + 16)
                if b.n:
                    pe.wait_ge(pre_act, 8 * b.n - 2)
                if b.n > 3:
                    pe.wait_ge(o_read, b.n - 3)
                for t in range(QT):
                    last = nc.tensor.transpose(work[:, t * P:(t + 1) * P], x_in[:, t, :], ident[:])
                last.then_inc(pre_ready, 1)

            def project_qk(b, j):
                pe.wait_ge(pre_act, 8 * b.n + 1 + 2 * j)
                nc.tensor.matmul(work[:], w_sb[:, j * C:(j + 1) * C], x_t[:], start=True, stop=True
                                 ).then_inc(pre_ready, 1)

            def project_v(b):
                pe.wait_ge(pre_act, 8 * b.n + 5)
                nc.tensor.matmul(work[:], ones[0:1, :], bias_v[0:1, :].unsqueeze(1).broadcast_to([1, QT, C]),
                                 start=True, stop=False)
                for t in range(QT):
                    last = nc.tensor.matmul(work[:, t * P:(t + 1) * P], x_t[:, t * P:(t + 1) * P],
                                            w_sb[:, 2 * C:3 * C], start=False, stop=t == QT - 1)
                last.then_inc(pre_ready, 1)

            def scores(b, r):
                p, h, qt = b.p, r // QT, r % QT
                if r == 0:
                    pe.wait_ge(stacks[p], 64 * b.pair + 64)
                pe.wait_ge(s_free, ROWSETS * b.n + r + 1)
                bank = s_ps[(b.n * ROWSETS + r) % SBANKS]
                w = (qt + 1) * P
                nc.tensor.matmul(bank[:, 0:w], q_st[p][0:KROWS, h * T + qt * P:h * T + qt * P + P],
                                 k_st[p][0:KROWS, h * T:h * T + w], start=True, stop=False)
                nc.tensor.matmul(bank[:, w - P:w], ident16[:], mask_q[:, T - P:T], start=False, stop=True
                                 ).then_inc(s_ready, 1)

            def count_short(b):
                pe.wait_ge(tau_ready, b.n + 1)
                pe.wait_ge(residual_read, b.n)
                nc.tensor.matmul(misc[0:1, 0:ROWSETS], ones_col[:], short[:], start=True, stop=True
                                 ).then_inc(short_counted, 1)

            def fix(b):
                pe.wait_ge(flags_ready, b.n + 1)

                def scores_to_fix(r):
                    p = b.p
                    take_turn(pe, fix_done)
                    pe.wait_ge(y_copied, b.n)
                    nc.tensor.matmul(misc[:], q_st[p][0:KROWS, bass.ds(r * P, P)],
                                     k_st[p][0:KROWS, bass.ds(r // QT * T, T)], start=True, stop=False)
                    nc.tensor.matmul(misc[:], ident16[:], mask_q[:, bass.ds((QT - 1 - r % QT) * P, T)],
                                     start=False, stop=True).then_inc(fix_scores, 1)
                    take_turn(pe, fix_tried)
                    nc.tensor.matmul(y_ps[0:1, 0:1], fix_open[:], ones_col[:], start=True, stop=True
                                     ).then_inc(fix_counted, 1)

                flagged_tiles(pe, scores_to_fix)

            def turn_tau(b):
                pe.wait_ge(tau_final, b.n + 1)
                nc.tensor.transpose(misc[0:ROWSETS, 0:P], neg_tau[:], ident[:]).then_inc(tau_turned, 1)

            def transposed(b, n, g, blk, tiles):
                p = b.p
                if n == 0:
                    pe.wait_ge(tau_rows, 48 * b.n + 48)
                if n == 1 and b.n > 1:
                    pe.wait_ge(o_copied, b.n - 1)
                if b.n or n > 1:
                    pe.wait_ge(p_ready, JOBS * b.n + n - 1)
                bank = t_ps[n % 2]
                col = 0
                for j, kt in tiles:
                    h, w = 4 * j + g, T - kt * P
                    nc.tensor.matmul(bank[:, col:col + w], k_st[p][0:KTAU, h * T + kt * P:h * T + kt * P + P],
                                     q_st[p][0:KTAU, h * T + kt * P:h * T + T], start=True, stop=False)
                    last = nc.tensor.matmul(bank[:, col:col + P], ident16[:], mask_k[:], start=False, stop=True)
                    col += w
                last.then_inc(t_ready, 1)

            def times_v(b, g, blk):
                pe.wait_ge(p_ready, JOBS * b.n + 10 * g + (4, 8, 10)[blk])
                if g == 0 and blk == 0:
                    pe.wait_ge(v_padded, b.n + 1)
                    pe.wait_ge(y_copied, b.n)
                for kt in ((0,), (1, 3), (2,))[blk]:
                    w, at = T - kt * P, 3 * P if kt == 3 else 0
                    for j in range(4):
                        last = nc.tensor.matmul(y_ps[32 * j:32 * j + 32, kt * P:T], v_pad[:, kt, 4 * j + g, :],
                                                p_t[blk][:, j, at:at + w],
                                                start=(g == 0 and blk == 0), stop=(g == 3 and blk == 2))
                last.then_inc(av_done, 1)

            def project_y(b):
                pe.wait_ge(y_copied, b.n + 1)
                pe.wait_ge(gates_copied, b.n)
                nc.tensor.matmul(misc[:], ones[0:1, :], bp_sb[0:1, :].unsqueeze(1).broadcast_to([1, QT, C]),
                                 start=True, stop=False)
                for t in range(QT):
                    last = nc.tensor.matmul(misc[:, t * P:(t + 1) * P], y_sb[:, t * P:(t + 1) * P], wp_sb[:],
                                            start=False, stop=t == QT - 1)
                last.then_inc(y_projected, 1)

            def turn_x1(b):
                pe.wait_ge(x1_ready, b.n + 1)
                if b.n + 1 < B:
                    pe.wait_ge(tau_act, 3 * (b.n + 1) + 2)
                for t in range(QT):
                    last = nc.tensor.transpose(misc[:, t * P:(t + 1) * P], x1[b.n % 3][:, t, :], ident[:])
                last.then_inc(x1_turned, 1)

            def logits(b):
                pe.wait_ge(x1_copied, b.n + 1)
                for t in range(QT):
                    last = nc.tensor.matmul(misc[:, t * NE:(t + 1) * NE], x1_t[:, t * P:(t + 1) * P], rw[:],
                                            start=True, stop=True)
                last.then_inc(logits_ready, 1)

            def turn_gates(b):
                pe.wait_ge(gates_ready, b.n + 1)
                nc.tensor.transpose(misc[0:QT * NE, 0:P], gates[:].rearrange("p t e -> p (t e)"), ident[:]
                                    ).then_inc(gates_turned, 1)

            def up(b, j):
                half, k = j // NJ, j % NJ
                if j == 0:
                    pe.wait_ge(o_read, b.n)
                    if b.n + 3 < B:
                        pe.wait_ge(pre_act, 8 * (b.n + 3) + 6)
                if j > 1:
                    pe.wait_ge(up_act, 2 * TILES * b.n + 2 * j - 2)
                bank = (work, t_ps[0])[j % 2]
                xs = x1_t[:, half * HALF:(half + 1) * HALF]
                nc.tensor.matmul(bank[:, 0:HALF], wu[:, k, :], xs, start=True, stop=True)
                nc.tensor.matmul(bank[:, HALF:T], wv[:, k, :], xs, start=True, stop=True).then_inc(up_ready, 1)

            def down(b, j):
                half, k = j // NJ, j % NJ
                pe.wait_ge(hid_ready, TILES * b.n + j + 1)
                if j == 0:
                    pe.wait_ge(o_copied, b.n)
                nc.tensor.matmul(o_ps[:, half * HALF:(half + 1) * HALF], wd[:, k, :], hid[j % (LAG + 1)][:],
                                 start=k == 0, stop=k == NJ - 1).then_inc(down_done, 1)

            def turn_out(b):
                pe.wait_ge(o_copied, b.n + 1)
                for t in range(QT):
                    last = nc.tensor.transpose(work[:, t * P:(t + 1) * P], o_t[:, t * P:(t + 1) * P], ident[:])
                last.then_inc(o_turned, 1)

            each(pe, dict(project_x=project_x, project_qk=project_qk, project_v=project_v, scores=scores,
                          count_short=count_short, fix=fix, turn_tau=turn_tau, transposed=transposed,
                          times_v=times_v, project_y=project_y, turn_x1=turn_x1, logits=logits,
                          turn_gates=turn_gates, up=up, down=down, turn_out=turn_out))

        @block.scalar
        def _(act):
            act.wait_ge(loaded, 16 * 13)
            nc.scalar.mul(bias_qk[:, 0:1], bias_qk[:, 0:1], SCALE).then_inc(consts2, 1)
            act.wait_ge(consts2, 2)

            def project_x(b):
                act.wait_ge(pre_ready, 4 * b.n + 1)
                nc.scalar.copy(x_t[:], work[:]).then_inc(pre_act, 1)

            def project_qk(b, j):
                act.wait_ge(pre_ready, 4 * b.n + 2 + j)
                if j == 0:
                    act.wait_ge(stored, 96 * b.n)
                scale = SCALE if j == 0 else 1.0
                for dst in (rest[j][:], parts[j][:, 0, :]):
                    nc.scalar.activation(dst, work[:], ACT.Identity, bias=bias_qk[:, j:j + 1], scale=scale
                                         ).then_inc(pre_act, 1)

            def project_v(b):
                act.wait_ge(pre_ready, 4 * b.n + 4)
                if b.n > 2:
                    act.wait_ge(v_padded, b.n - 2)
                nc.scalar.copy(v_nat[b.n % 3][:].rearrange("p t c -> p (t c)"), work[:]).then_inc(pre_act, 1)

            def second_parts(b):
                for j in range(2):
                    act.wait_ge(pre_pool, 4 * b.n + j + 1)
                    nc.scalar.copy(parts[j][:, 1, :], rest[j][:]).then_inc(pre_act, 1)

            def turn_tau(b):
                act.wait_ge(tau_turned, b.n + 1)
                act.wait_ge(tau_pool, 2 * b.n)
                nc.scalar.copy(tau_t[:], misc[0:ROWSETS, 0:P]).then_inc(tau_act, 1)
                act.wait_ge(tau_rows, 48 * b.n)
                nc.scalar.copy(tau_parts[:, 0, :], misc[0:ROWSETS, 0:P]).then_inc(tau_act, 1)
                act.wait_ge(tau_pool, 2 * b.n + 1)
                nc.scalar.copy(tau_parts[:, 1, :], tau_rest[:]).then_inc(tau_act, 1)

            def transposed(b, n, g, blk, tiles):
                if b.n or g:
                    act.wait_ge(av_done, 12 * b.n + 3 * g + blk - 2)
                act.wait_ge(t_ready, JOBS * b.n + n + 1)
                j = tiles[0][0]
                if blk == 2:
                    dst, src = p_t[2][:, j:j + 2, :], t_ps[n % 2][:].rearrange("p (a n) -> p a n", a=2)
                else:
                    dst, src = p_t[blk][:, j, :], t_ps[n % 2][:]
                nc.scalar.activation(dst, src, ACT.Relu).then_inc(p_ready, 1)

            def copy_y(b):
                act.wait_ge(av_done, 12 * b.n + 12)
                act.wait_ge(y_projected, b.n)
                nc.scalar.copy(y_sb[:], y_ps[:]).then_inc(y_copied, 1)

            def turn_x1(b):
                act.wait_ge(x1_turned, b.n + 1)
                act.wait_ge(up_ready, TILES * b.n)
                nc.scalar.copy(x1_t[:], misc[:]).then_inc(x1_copied, 1)

            def softmax(b):
                act.wait_ge(route_step, ROUTE * b.n + 2)
                nc.scalar.activation(score[:], score[:], ACT.Exp).then_inc(exped, 1)

            def turn_gates(b):
                act.wait_ge(gates_turned, b.n + 1)
                act.wait_ge(gates_stored, 16 * b.n)
                nc.scalar.copy(g_t[:], misc[0:QT * NE, 0:P]).then_inc(gates_copied, 1)

            def up(b, j):
                act.wait_ge(up_ready, TILES * b.n + j + 1)
                if b.n or j > 1:
                    act.wait_ge(hid_ready, TILES * b.n + j - 1)
                bank = (work, t_ps[0])[j % 2]
                nc.scalar.activation(silu[j % 2][:], bank[:, 0:HALF], ACT.Silu).then_inc(up_act, 1)
                nc.scalar.copy(lin[j % 2][:], bank[:, HALF:T]).then_inc(up_act, 1)

            def copy_out(b):
                act.wait_ge(down_done, TILES * b.n + TILES)
                act.wait_ge(o_turned, b.n)
                nc.scalar.copy(o_t[:], o_ps[:]).then_inc(o_copied, 1)

            each(act, dict(project_x=project_x, project_qk=project_qk, project_v=project_v,
                           second_parts=second_parts, turn_tau=turn_tau, transposed=transposed,
                           copy_y=copy_y, turn_x1=turn_x1, softmax=softmax, turn_gates=turn_gates, up=up,
                           copy_out=copy_out))

        @block.vector
        def _(dve):
            dve.wait_ge(consts, CONSTS)
            dve.wait_ge(consts2, 1)
            dve.wait_ge(loaded, 16 * 13)

            def chain(sem, b, per):
                n = [0]

                def link(ins):
                    n[0] += 1
                    assert n[0] <= per
                    ins.then_inc(sem, 1)
                    dve.wait_ge(sem, per * b.n + n[0])
                return link

            def scores(b, r):
                dve.wait_ge(s_ready, ROWSETS * b.n + r + 1)
                w = (r % QT + 1) * P
                chunks = s_ps[(b.n * ROWSETS + r) % SBANKS][:, 0:w].rearrange("p (n c) -> p c n", c=CH)
                for k in range(CH):
                    last = nc.vector.max(top[:, r, k, :], chunks[:, k, :])
                last.then_inc(s_free, 1)

            def by_rows(ap):
                return ap.rearrange("p (r i) -> p r i", i=2 * TOP)

            def every_row(table):
                return table[:].unsqueeze(1).broadcast_to([P, ROWSETS, 2 * TOP])

            def thresholds(b):
                link = chain(sort_step, b, SORT)
                dve.wait_ge(s_free, ROWSETS * b.n + SBANKS + ROWSETS)

                def exchange(dst, src, size, stride, count):
                    s = src[:, 0:count].rearrange("p (g a s) -> p g a s", a=2, s=stride)
                    d = dst[:, 0:count].rearrange("p (g a s) -> p g a s", a=2, s=stride)
                    nc.vector.tensor_tensor(d[:, :, 0, :], s[:, :, 0, :], s[:, :, 1, :], ALU.max)
                    link(nc.vector.tensor_tensor(d[:, :, 1, :], s[:, :, 0, :], s[:, :, 1, :], ALU.min))

                pairs = top[:].rearrange("p r (m a) i -> p (r m) a i", a=2)
                merged = m_a[:].rearrange("p (g a i) -> p g a i", a=2, i=TOP)
                nc.vector.tensor_tensor(merged[:, :, 0, :], pairs[:, :, 0, :], pairs[:, :, 1, ::-1], ALU.max)
                link(nc.vector.tensor_tensor(merged[:, :, 1, :], pairs[:, :, 0, :], pairs[:, :, 1, ::-1], ALU.min))
                exchange(m_b, m_a, TOP, 4, ROWSETS * CH * TOP)
                exchange(m_a, m_b, TOP, 2, ROWSETS * CH * TOP)
                exchange(m_b, m_a, TOP, 1, ROWSETS * CH * TOP)
                two = m_b[:].rearrange("p (r m i) -> p r m i", m=2, i=2 * TOP)
                kept = ROWSETS * 2 * TOP
                link(nc.vector.tensor_tensor(m_a[:, 0:kept].rearrange("p (r i) -> p r i", i=2 * TOP),
                                             two[:, :, 0, :], two[:, :, 1, ::-1], ALU.max))
                exchange(m_b, m_a, 2 * TOP, 8, kept)
                exchange(m_a, m_b, 2 * TOP, 4, kept)
                exchange(m_b, m_a, 2 * TOP, 2, kept)
                exchange(m_a, m_b, 2 * TOP, 1, kept)
                ranked = m_a[:, 0:kept]
                prefix = m_b[:, 0:kept]
                link(nc.vector.tensor_tensor_scan(prefix, restart[:].rearrange("p r i -> p (r i)"), ranked, 0.0,
                                                  ALU.mult, ALU.add))
                link(nc.vector.scalar_tensor_tensor(out=by_rows(prefix), in0=by_rows(prefix), scalar=1.0,
                                                    in1=every_row(recip_k), op0=ALU.subtract, op1=ALU.mult))
                nc.vector.tensor_reduce(tau[:], prefix.rearrange("p (r i) -> p r i", i=2 * TOP), AX, ALU.max)
                link(nc.vector.tensor_reduce(last_kept[:], top[:, :, :, TOP - 1], AX, ALU.max))
                link(nc.vector.tensor_tensor(last_kept[:], last_kept[:],
                                             ranked.rearrange("p (r i) -> p r i", i=2 * TOP)[:, :, 2 * TOP - 1],
                                             ALU.max))
                nc.vector.tensor_tensor(short[:], last_kept[:], tau[:], ALU.is_gt).then_inc(tau_ready, 1)

            def flags(b):
                link = chain(flag_step, b, 3)
                dve.wait_ge(short_counted, b.n + 1)
                dve.wait_ge(tau_ready, b.n + 1)
                link(nc.vector.tensor_scalar(short_any[:], misc[0:1, 0:ROWSETS], 0.5, None, ALU.is_gt))
                nc.vector.tensor_copy(short_i[:], short_any[:])
                nc.vector.tensor_tensor(from_end[:], short_any[:], countdown[:], ALU.mult)
                link(nc.vector.tensor_reduce(total[:], short_any[:], AX, ALU.add))
                nc.vector.tensor_scalar(plan_i[0:1, 0:1], total[:], float(TOP), None, ALU.min)
                nc.vector.tensor_scalar(plan_i[0:1, 1:2], total[:], float(TOP), None, ALU.is_gt)
                link(nc.vector.max(first_few[:], from_end[:]))
                nc.vector.tensor_scalar(list_i[:], first_few[:], -1.0, float(ROWSETS), ALU.mult, ALU.add
                                        ).then_inc(flags_ready, 1)
                dve.wait_ge(flags_ready, b.n + 1)

            def newton_step():
                nc.vector.scalar_tensor_tensor(out=fix_over[:], in0=misc[:], scalar=fix_tau[:, 0:1], in1=zeros[:],
                                               op0=ALU.subtract, op1=ALU.max, accum_out=fix_sum[:, 0:1])
                nc.vector.tensor_scalar(fix_over2[:], misc[:], fix_tau[:, 0:1], 0.0,
                                        ALU.is_gt, ALU.add, accum_out=fix_sum[:, 1:2])
                dve.drain()
                nc.vector.reciprocal(fix_sum[:, 1:2], fix_sum[:, 1:2])
                nc.vector.tensor_scalar(fix_sum[:, 0:1], fix_sum[:, 0:1], 1.0, None, ALU.subtract)
                dve.drain()
                nc.vector.scalar_tensor_tensor(out=fix_tau[:], in0=fix_sum[:, 0:1], scalar=fix_sum[:, 1:2],
                                               in1=fix_tau[:], op0=ALU.mult, op1=ALU.add)
                dve.drain()

            def fix(r):
                nc.vector.tensor_copy(fix_tau[:], tau[:, bass.ds(r, 1)])
                take_turn(dve, fix_scores)
                dve.drain()
                with dve.Fori(0, FEW):
                    newton_step()
                nc.vector.tensor_scalar(fix_open[:], fix_sum[:, 0:1], CLOSE, None, ALU.is_gt
                                        ).then_inc(fix_tried, 1)
                take_turn(dve, fix_counted)
                nc.vector.tensor_copy(open_i[:], y_ps[0:1, 0:1])
                dve.drain()
                still = dve.value_load(open_i[0:1, 0:1], min_val=0, max_val=P)
                with dve.If(still):
                    with dve.Fori(0, NEWTON - FEW):
                        newton_step()
                nc.vector.tensor_copy(tau[:, bass.ds(r, 1)], fix_tau[:]).then_inc(fix_done, 1)
                dve.drain()

            def fix_thresholds(b):
                flagged_tiles(dve, fix)
                nc.vector.tensor_scalar(neg_tau[:], tau[:], -1.0, None, ALU.mult).then_inc(tau_final, 1)

            def normalise_moments(link, total, stats, moments):
                for t in range(QT):
                    last = nc.vector.bn_stats(stats[:, t, :], total[:, t, :])
                link(last)
                for t in range(QT):
                    last = nc.vector.bn_aggr(moments[:, t, :], stats[:, t, :])
                link(last)

            def residual(b):
                dve.wait_ge(y_projected, b.n + 1)
                dve.wait_ge(res_loaded, 16 * b.n + 16)
                nc.vector.tensor_tensor(summed[:], misc[:].rearrange("p (t c) -> p t c", c=C), x_res[:],
                                        ALU.add).then_inc(residual_read, 1)
                dve.wait_ge(residual_read, b.n + 1)
                normalise_moments(chain(norm_step, b, NORM), summed, stats, moments)

            def scale_x1(b):
                dve.wait_ge(rstd_ready, b.n + 1)
                for t in range(QT):
                    last = nc.vector.tensor_scalar(x1[b.n % 3][:, t, :], summed[:, t, :],
                                                   moments[:, t, 0:1], rstd[:, t:t + 1], ALU.subtract, ALU.mult)
                last.then_inc(x1_ready, 1)
                dve.wait_ge(x1_ready, b.n + 1)

            def over_experts(ap):
                return ap.unsqueeze(2).broadcast_to([P, QT, NE])

            def over_tiles(ap):
                return ap.unsqueeze(1).broadcast_to([P, QT, NE])

            route_link = [None]

            def softmax(b):
                link = route_link[0] = chain(route_step, b, ROUTE)
                lg = misc[:, 0:QT * NE].rearrange("p (t e) -> p t e", e=NE)
                dve.wait_ge(logits_ready, b.n + 1)
                link(nc.vector.tensor_reduce(most[:], lg, AX, ALU.max))
                link(nc.vector.tensor_tensor(score[:], lg, over_experts(most[:]), ALU.subtract))

            def choose(b):
                link = route_link[0]
                dve.wait_ge(exped, b.n + 1)
                link(nc.vector.tensor_reduce(most[:], score[:], AX, ALU.add))
                link(nc.vector.reciprocal(most[:], most[:]))
                link(nc.vector.tensor_tensor(score[:], score[:], over_experts(most[:]), ALU.mult))
                link(nc.vector.tensor_tensor(biased[:], score[:], over_tiles(bias_e[:]), ALU.add))
                for k in range(2):
                    link(nc.vector.tensor_reduce(most[:], biased[:], AX, ALU.max))
                    link(nc.vector.tensor_tensor(equal[:], biased[:], over_experts(most[:]), ALU.is_equal))
                    link(nc.vector.tensor_tensor(equal[:], equal[:], over_tiles(order[:]), ALU.mult))
                    link(nc.vector.tensor_reduce(most[:], equal[:], AX, ALU.max))
                    last = nc.vector.tensor_tensor(chosen[k][:], equal[:], over_experts(most[:]), ALU.is_equal)
                    if k == 0:
                        link(last)
                        link(nc.vector.scalar_tensor_tensor(out=biased[:], in0=chosen[0][:], scalar=MASKED,
                                                            in1=biased[:], op0=ALU.mult, op1=ALU.add))
                link(last)
                link(nc.vector.tensor_tensor(gates[:], chosen[0][:], chosen[1][:], ALU.add))
                nc.vector.tensor_tensor(gates[:], gates[:], score[:], ALU.mult).then_inc(gates_ready, 1)
                dve.wait_ge(gates_ready, b.n + 1)

            def sum_out(b):
                dve.wait_ge(o_turned, b.n + 1)
                dve.wait_ge(sent, 16 * b.n)
                nc.vector.tensor_tensor(f_summed[:], work[:].rearrange("p (t c) -> p t c", c=C), x1[b.n % 3][:],
                                        ALU.add).then_inc(o_read, 1)
                dve.wait_ge(o_read, b.n + 1)
                normalise_moments(chain(f_norm_step, b, NORM), f_summed, f_stats, f_moments)

            def scale_out(b):
                dve.wait_ge(f_rstd_ready, b.n + 1)
                for t in range(QT):
                    last = nc.vector.tensor_scalar(f_summed[:, t, :], f_summed[:, t, :], f_moments[:, t, 0:1],
                                                   f_rstd[:, t:t + 1], ALU.subtract, ALU.mult)
                last.then_inc(result_ready, 1)
                dve.wait_ge(result_ready, b.n + 1)

            each(dve, dict(scores=scores, sort=thresholds, flags=flags, fix=fix_thresholds, residual=residual,
                           scale_x1=scale_x1, softmax=softmax, gates=choose, sum_out=sum_out,
                           scale_out=scale_out))


_INS = ["L0_attn_x", "L0_attn_w_attn", "L0_attn_b_attn", "L0_attn_w_proj", "L0_attn_b_proj",
        "L0_ffn_router_w", "L0_ffn_expert_bias", "L0_ffn_w1", "L0_ffn_w2", "L0_ffn_w3",
        "L0_ffn_sw1", "L0_ffn_sw2", "L0_ffn_sw3"]


def kernel(**inputs):
    import numpy as _np
    import concourse.bacc as _bacc
    from concourse import mybir as _mybir
    from concourse.bass_utils import run_bass_kernel_spmd as _run

    nc = _bacc.Bacc("TRN2", target_bir_lowering=False, num_devices=1)
    arrays, args = {}, []
    for name in _INS:
        a = _np.ascontiguousarray(inputs[name])
        arrays[f"in_{name}"] = a
        args.append(nc.dram_tensor(f"in_{name}", a.shape, _mybir.dt.from_np(a.dtype), kind="ExternalInput").ap())
    args.append(nc.dram_tensor("out_0", (B, T, C), _mybir.dt.float32, kind="ExternalOutput").ap())
    program(nc, *args)
    r = _run(nc, [arrays], core_ids=[0])
    return r.results[0]["out_0"]
```

```python
import concourse.bass as bass
from concourse import mybir
from contextlib import ExitStack

F32 = mybir.dt.float32
BF16 = mybir.dt.bfloat16
I32 = mybir.dt.int32
ALU = mybir.AluOpType
ACT = mybir.ActivationFunctionType
AX = mybir.AxisListType.X

B, T, C = 8, 512, 128
H = 16
HD = C // H
P = 128
QT = T // P
NT = B * QT
NE = 8
PARTS = 3
KROWS = PARTS * PARTS * HD
KTAU = KROWS + PARTS
ROWSETS = H * QT
CH = 4
TOP = 8
NJ = NE + 1
HALF = T // 2
TILES = 2 * NJ
LAG = 2
SLACK = -0.1
EARLY = 2.2
TAU_LATENCY = 8.1
TRANSPOSED_WAIT = 0.58
RELU = 0.65
BEHIND = 3
NORM = 2
SORT = 13
ROUTE = 19
MASKED = -1e30
EPS = 1e-5
SBANKS = 3
NEWTON = 24
FEW = 3
CLOSE = 3e-6
JOBS = 40
SCALE = 1.0 / float(HD) ** 0.5


class Batch:

    def __init__(self, n):
        self.n, self.pair, self.p = n, n // 2, n % 2


BATCHES = [Batch(n) for n in range(B)]


def tiles_of_transposed(g):
    for j in range(4):
        yield 0, [(j, 0)]
    for j in range(4):
        yield 1, [(j, 1), (j, 3)]
    for j in (0, 2):
        yield 2, [(j, 2), (j + 1, 2)]


class Order:

    PE = dict(up=0.85, down=0.43, transposed=0.22, turn_out=0.9, turn_x1=0.9, logits=1.7, project_x=0.9,
              project_qk=0.85, project_v=1.7, project_y=1.7, turn_gates=0.2, count_short=0.1, turn_tau=0.2)
    DVE = dict(sort=22.5, residual=2.2, sum_out=2.2, flags=1.2, route=0.1, fix=1.3)
    SCORES_PE, SCORES_DVE = 0.054, 0.13
    SCORES_PE0, SCORES_DVE0 = 0.05, 0.307
    TIMES_V = (0.92, 0.92, 0.43)
    EXPERT_POOL = 1.4

    def __init__(self):
        self.items = []
        self.pe = self.dve = self.pool = self.act = 0.0
        self.relu = [0.0, 0.0]
        self.banks = [0.0] * SBANKS
        self.hidden = []
        self.batch, self.row = None, 0
        self.before_sort = ()

    def add(self, kind, b, *args):
        if b is None:
            return
        self.items.append((kind, b) + args)
        if kind == "scores":
            keys = args[0] % QT + 1
            self.pe = max(self.pe, self.banks[0]) + self.SCORES_PE * keys + self.SCORES_PE0
            self.dve = max(self.dve, self.pe) + self.SCORES_DVE * keys + self.SCORES_DVE0
            self.banks = self.banks[1:] + [self.dve]
            return
        if kind == "up":
            self.pool = max(self.pool, self.pe + 1.4) + self.EXPERT_POOL
            self.hidden.append(self.pool)
        elif kind == "down":
            self.pe = max(self.pe, self.hidden.pop(0))
        elif kind == "transposed":
            self.pe = max(self.pe, self.relu[0])
            self.act = max(self.act, self.pe + TRANSPOSED_WAIT) + RELU
            self.relu = [self.relu[1], self.act]
        elif kind == "times_v":
            self.pe += self.TIMES_V[args[1]]
        self.pe += self.PE.get(kind, 0.0)
        self.dve += self.DVE.get(kind, 0.0)

    def scores_of(self, b):
        self.batch, self.row = b, 0

    def scores(self, n=1):
        for _ in range(n):
            if self.batch and self.row < ROWSETS:
                self.add("scores", self.batch, self.row)
                self.row += 1
                if self.row == ROWSETS:
                    for _ in self.before_sort:
                        pass
                    self.add("sort", self.batch)

    def fill(self):
        ready = max(self.pe, self.relu[0]) + SLACK
        while self.batch and self.row < ROWSETS and self.banks[0] <= ready:
            self.scores()
            ready = max(self.pe, self.relu[0]) + SLACK


def schedule():
    def known(n):
        return BATCHES[n] if 0 <= n < B else None

    order = Order()
    add = order.add

    def project(b):
        yield add("project_x", b)
        yield add("project_qk", b, 0)
        yield add("project_qk", b, 1)
        yield add("project_v", b)
        add("second_parts", b)
        yield add("store_parts", b)

    def choose(b):
        yield add("turn_x1", b)
        yield None
        yield add("logits", b)
        yield None
        yield add("route", b, 0)
        add("route", b, 1)
        yield add("softmax", b)
        yield None
        for step in range(2, ROUTE):
            yield add("route", b, step)
        yield add("turn_gates", b)

    def experts(b):
        for j in range(TILES + LAG):
            if j < TILES:
                add("up", b, j)
            if j >= LAG:
                add("down", b, j - LAG)
            yield

    def attention(b):
        waiting = []
        n = 0
        for g in range(4):
            for block, parts in tiles_of_transposed(g):
                add("transposed", b, n, g, block, parts)
                n += 1
                if waiting and n - waiting[0][1] > BEHIND:
                    add("times_v", b, *waiting.pop(0)[0])
                if n % 10 in (4, 8, 0):
                    waiting.append(((g, block), n))
                    add("mask", b, g, block)
                yield
        for block, _ in waiting:
            add("times_v", b, *block)

    for _ in project(BATCHES[0]):
        pass
    add("load_stacks", BATCHES[0])
    for s in range(-1, B + 2):
        c, b, f, o, p = known(s + 1), known(s), known(s - 1), known(s - 2), known(s + 2)
        order.scores_of(c)
        if s != B:
            expert = experts(o)
        if o and s < B:
            while order.pe < order.dve - EARLY and next(expert, True) is None:
                pass
        add("count_short", b)
        order.pe = max(order.pe, order.dve)
        add("residual", f)
        add("flags", b)
        next(expert, None)
        if b:
            order.scores(2)
        add("fix", b)
        order.pe = max(order.pe, order.dve)
        add("turn_tau", b)
        tau_sent = order.pe + TAU_LATENCY
        for _ in expert:
            order.fill()
        add("scale_x1", f)
        add("pad_v", b)
        add("load_residual", b)
        add("bias_residual", b)
        while b and c and order.pe < tau_sent and order.row < ROWSETS:
            order.scores()
        order.fill()
        add("copy_out", o)
        chosen, projected = choose(f), project(p)
        order.before_sort = chosen
        if s == B - 1:
            add("turn_out", o)
            add("sum_out", o)
            expert = experts(f)
            for _ in range(12):
                next(chosen, None)
            for n, _ in enumerate(attention(b)):
                if n == 12:
                    add("scale_out", o)
                next(chosen, None)
                if next(chosen, True):
                    next(expert, None)
        else:
            for n, _ in enumerate(attention(b)):
                order.fill()
                if n == 1:
                    add("turn_out", o)
                elif n == 3:
                    add("sum_out", o)
                elif n == 12:
                    add("scale_out", o)
                if n > 6 and n % 5 == 0:
                    next(projected, None)
                if n > 3:
                    next(chosen, None)
        for _ in projected:
            pass
        for _ in chosen:
            pass
        order.scores(ROWSETS)
        add("copy_y", b)
        add("project_y", b)
        add("load_stacks", p)
    return order.items


def program(nc, x, w_attn, b_attn, w_proj, b_proj, router_w, expert_bias, w1, w2, w3, sw1, sw2, sw3, out):
    q_parts = nc.dram_tensor("q_parts", (B, PARTS, C, T), BF16).ap()
    k_parts = nc.dram_tensor("k_parts", (B, PARTS, C, T), BF16).ap()
    gates_dram = nc.dram_tensor("gates_t", (NT * NE, P), F32).ap()
    ctx = ExitStack()
    with ctx:
        def sb(name, shape, dt=F32):
            return ctx.enter_context(nc.sbuf_tensor(name, shape, dt))

        def ps(name):
            return ctx.enter_context(nc.psum_tensor(name, [P, T], F32))

        def sem(name):
            return ctx.enter_context(nc.semaphore(name))

        ident = sb("ident", [P, P])
        ident16 = sb("ident16", [P, P], BF16)
        mask_q = sb("mask_q", [P, 2 * T - P], BF16)
        ones_col = sb("ones_col", [P, 1], BF16)
        zeros = sb("zeros", [P, T], BF16)
        restart = sb("restart", [P, ROWSETS, 2 * TOP], BF16)
        recip_k = sb("recip_k", [P, 2 * TOP])
        countdown = sb("countdown", [1, ROWSETS])
        minus_half = sb("minus_half", [P, QT])
        order = sb("order", [P, NE])
        w_sb = sb("w_sb", [P, 3 * C])
        bias_qk = sb("bias_qk", [P, 2])
        bias_v = sb("bias_v", [P, C])
        wp_sb = sb("wp_sb", [P, C])
        bias_y = sb("bias_y", [P, C])
        rw = sb("rw", [P, NE])
        bias_e = sb("bias_e", [P, NE])
        wu = sb("wu", [P, NJ, C])
        wv = sb("wv", [P, NJ, C])
        wd = sb("wd", [P, NJ, C])
        x_in = sb("x_in", [P, QT, C])
        x_t = sb("x_t", [P, T])
        rest = [sb(f"rest{j}", [P, T]) for j in range(2)]
        parts = [sb(f"parts{j}", [P, PARTS, T], BF16) for j in range(2)]
        v_nat = [sb(f"v_nat{i}", [P, QT, C]) for i in range(3)]
        q_st = [sb(f"q_st{i}", [KTAU, H * T], BF16) for i in range(2)]
        k_st = [sb(f"k_st{i}", [P, H * T], BF16) for i in range(2)]
        v_pad = sb("v_pad", [P, QT, H, 32])
        p_t = [sb("p_t0", [P, 4, T]), sb("p_t1", [P, 4, T]), sb("p_t2", [P, 4, 2 * P])]
        top = sb("top", [P, ROWSETS, CH, TOP])
        m_a = sb("m_a", [P, ROWSETS * CH * TOP])
        m_b = sb("m_b", [P, ROWSETS * CH * TOP])
        tau = sb("tau", [P, ROWSETS])
        neg_tau = sb("neg_tau", [P, ROWSETS])
        last_kept = sb("last_kept", [P, ROWSETS])
        short = sb("short", [P, ROWSETS], BF16)
        short_any = sb("short_any", [1, ROWSETS])
        from_end = sb("from_end", [1, ROWSETS])
        first_few = sb("first_few", [1, TOP])
        total = sb("total", [1, 1])
        plan_i = sb("plan_i", [1, 2], I32)
        list_i = sb("list_i", [1, TOP], I32)
        short_i = sb("short_i", [1, ROWSETS], I32)
        fix_tau = sb("fix_tau", [P, 1])
        fix_sum = sb("fix_sum", [P, 2])
        fix_over = sb("fix_over", [P, T], BF16)
        fix_over2 = sb("fix_over2", [P, T], BF16)
        fix_open = sb("fix_open", [P, 1], BF16)
        open_i = sb("open_i", [1, 1], I32)
        tau_t = sb("tau_t", [ROWSETS, P])
        tau_rest = sb("tau_rest", [ROWSETS, P])
        tau_parts = sb("tau_parts", [ROWSETS, PARTS, P], BF16)
        y_sb = sb("y_sb", [P, T])
        x_res = sb("x_res", [P, QT, C])
        summed = sb("summed", [P, QT, C])
        stats = sb("stats", [P, QT, 6])
        moments = sb("moments", [P, QT, 2])
        shifted = sb("shifted", [P, QT])
        minus_mean = sb("minus_mean", [P, QT])
        rstd = sb("rstd", [P, QT])
        x1 = [sb(f"x1_{i}", [P, QT, C]) for i in range(3)]
        x1_t = sb("x1_t", [P, T])
        score = sb("score", [P, QT, NE])
        biased = sb("biased", [P, QT, NE])
        equal = sb("equal", [P, QT, NE])
        chosen = [sb(f"chosen{k}", [P, QT, NE]) for k in range(2)]
        most = sb("most", [P, QT])
        gates = sb("gates", [P, QT, NE])
        g_t = sb("g_t", [QT * NE, P])
        gate = [sb(f"gate{i}", [P, QT // 2, NE, P]) for i in range(2)]
        silu = [sb(f"silu{i}", [P, HALF]) for i in range(2)]
        lin = [sb(f"lin{i}", [P, HALF]) for i in range(2)]
        hid = [sb(f"hid{i}", [P, HALF]) for i in range(LAG + 1)]
        o_t = sb("o_t", [P, T])
        f_summed = sb("f_summed", [P, QT, C])
        f_stats = sb("f_stats", [P, QT, 6])
        f_moments = sb("f_moments", [P, QT, 2])
        f_shifted = sb("f_shifted", [P, QT])
        f_minus_mean = sb("f_minus_mean", [P, QT])
        f_rstd = sb("f_rstd", [P, QT])

        s_ps = [ps(f"s_ps{i}") for i in range(SBANKS)]
        t_ps = [ps(f"t_ps{i}") for i in range(2)]
        y_ps = ps("y_ps")
        misc = ps("misc")
        work = ps("work")

        consts = sem("consts")
        rows_of_ones = sem("rows_of_ones")
        v_zeroed = sem("v_zeroed")
        bias_scaled = sem("bias_scaled")
        first_loaded = sem("first_loaded")
        loaded = sem("loaded")
        x_loaded = sem("x_loaded")
        pre_ready = sem("pre_ready")
        pre_act = sem("pre_act")
        pre_pool = sem("pre_pool")
        stored = sem("stored")
        stacks = [sem(f"stacks{i}") for i in range(2)]
        tau_rows = sem("tau_rows")
        s_ready = sem("s_ready")
        s_free = sem("s_free")
        sort_step = sem("sort_step")
        tau_ready = sem("tau_ready")
        short_counted = sem("short_counted")
        flag_step = sem("flag_step")
        flags_ready = sem("flags_ready")
        fix_scores = sem("fix_scores")
        fix_tried = sem("fix_tried")
        fix_counted = sem("fix_counted")
        fix_done = sem("fix_done")
        tau_final = sem("tau_final")
        tau_turned = sem("tau_turned")
        tau_act = sem("tau_act")
        tau_pool = sem("tau_pool")
        t_ready = sem("t_ready")
        p_ready = sem("p_ready")
        p_masked = sem("p_masked")
        av_done = sem("av_done")
        v_padded = sem("v_padded")
        y_copied = sem("y_copied")
        y_projected = sem("y_projected")
        res_loaded = sem("res_loaded")
        res_biased = sem("res_biased")
        residual_read = sem("residual_read")
        norm_step = sem("norm_step")
        var_shifted = sem("var_shifted")
        rstd_ready = sem("rstd_ready")
        x1_ready = sem("x1_ready")
        x1_turned = sem("x1_turned")
        x1_copied = sem("x1_copied")
        logits_ready = sem("logits_ready")
        route_step = sem("route_step")
        exped = sem("exped")
        gates_turned = sem("gates_turned")
        gates_copied = sem("gates_copied")
        gates_stored = sem("gates_stored")
        gate_loaded = [sem(f"gate_loaded{i}") for i in range(2)]
        up_ready = sem("up_ready")
        up_act = sem("up_act")
        gate_step = sem("gate_step")
        product_ready = sem("product_ready")
        hid_ready = sem("hid_ready")
        down_done = sem("down_done")
        o_copied = sem("o_copied")
        o_turned = sem("o_turned")
        o_read = sem("o_read")
        f_norm_step = sem("f_norm_step")
        f_var_shifted = sem("f_var_shifted")
        f_rstd_ready = sem("f_rstd_ready")
        result_ready = sem("result_ready")
        sent = sem("sent")
        block = ctx.enter_context(nc.Block())

        items = schedule()
        CONSTS = 13
        LATER_LOADS = 11

        def each(eng, parts_of):
            for kind, b, *args in items:
                if kind in parts_of:
                    parts_of[kind](b, *args)

        def banks_of_experts(b):
            if b.n >= B - 2:
                return s_ps[0], s_ps[1], s_ps[2]
            return work, t_ps[0], t_ps[1]

        def flagged_tiles(eng, body):
            listed = eng.value_load(plan_i[0:1, 0:1], min_val=0, max_val=TOP)
            with eng.If(listed):
                with eng.Fori(0, listed) as i:
                    body(eng.value_load(list_i[0:1, bass.ds(i, 1)], min_val=0, max_val=ROWSETS - 1))
                more = eng.value_load(plan_i[0:1, 1:2], min_val=0, max_val=1)
                with eng.If(more):
                    with eng.Fori(0, ROWSETS) as r:
                        flag = eng.value_load(short_i[0:1, bass.ds(r, 1)], min_val=0, max_val=1)
                        with eng.If(flag):
                            body(r)

        def take_turn(eng, sem):
            eng.wait_ge(sem, 1)
            eng.sem_clear(sem)

        @block.sync
        def _(sp):
            def load_x(b):
                sp.dma_start(x_in[:], x[b.n].rearrange("(t p) c -> p t c", p=P)).then_inc(x_loaded, 16)

            load_x(BATCHES[0])
            sp.dma_start(w_sb[:], w_attn).then_inc(first_loaded, 16)
            sp.dma_start(bias_qk[:], b_attn[0:2 * C].rearrange("(j p) -> p j", p=P),
                         allow_slow_non_contiguous=True).then_inc(first_loaded, 16)
            sp.dma_start(bias_v[:], b_attn[2 * C:3 * C].partition_broadcast(P)).then_inc(loaded, 16)
            sp.dma_start(wp_sb[:], w_proj).then_inc(loaded, 16)
            sp.dma_start(bias_y[:], b_proj.partition_broadcast(P)).then_inc(loaded, 16)
            sp.dma_start(rw[:], router_w).then_inc(loaded, 16)
            sp.dma_start(bias_e[:], expert_bias.partition_broadcast(P)).then_inc(loaded, 16)
            for dst, shared, routed in ((wu, sw1, w1), (wv, sw3, w3), (wd, sw2, w2)):
                sp.dma_start(dst[:, 0, :], shared).then_inc(loaded, 16)
                sp.dma_start(dst[:, 1:NJ, :], routed.rearrange("e p n -> p e n")).then_inc(loaded, 16)

            def project_x(b):
                if b.n + 1 < B:
                    sp.wait_ge(pre_ready, 4 * b.n + 1)
                    load_x(BATCHES[b.n + 1])

            def store_parts(b):
                for i in range(PARTS):
                    if i == 0:
                        sp.wait_ge(pre_act, 8 * b.n + 5)
                    elif i == 1:
                        sp.wait_ge(pre_act, 8 * b.n + 8)
                    else:
                        sp.wait_ge(pre_pool, 4 * b.n + 4)
                    for j, dst in enumerate((q_parts, k_parts)):
                        to = bass.AP(dst.tensor, (b.n * PARTS + i) * (C * T), [[T, H], [H * T, HD], [1, T]])
                        sp.dma_start(to, parts[j][:, i, :]).then_inc(stored, 16)

            def load_stacks(b):
                sp.wait_ge(stored, 96 * b.n + 96)
                if b.n < 2:
                    sp.wait_ge(rows_of_ones, b.n + 1)
                else:
                    sp.wait_ge(av_done, 12 * (b.n - 2) + 12)
                p = b.p
                base = b.n * (PARTS * C * T)
                for u in range(PARTS):
                    src = bass.AP(q_parts.tensor, base + u * C * T, [[0, PARTS], [H * T, HD], [1, H * T]])
                    sp.dma_start(q_st[p][24 * u:24 * u + 24, :], src).then_inc(stacks[p], 16)
                src = bass.AP(k_parts.tensor, base, [[0, PARTS], [H * T, PARTS * HD], [1, H * T]])
                sp.dma_start(k_st[p][0:KROWS, :], src).then_inc(stacks[p], 16)

            def turn_tau(b):
                sp.wait_ge(tau_pool, 2 * b.n + 2)
                for i in range(PARTS):
                    sp.dma_start(q_st[b.p][KROWS + i:KROWS + i + 1, :].rearrange("a (r t) -> a r t", t=P),
                                 tau_parts[:, i, :]).then_inc(tau_rows, 16)

            def load_residual(b):
                sp.wait_ge(residual_read, b.n)
                sp.dma_start(x_res[:], x[b.n].rearrange("(t p) c -> p t c", p=P)).then_inc(res_loaded, 16)

            def turn_gates(b):
                sp.wait_ge(gates_copied, b.n + 1)
                rows = QT * NE
                sp.dma_start(gates_dram[b.n * rows:(b.n + 1) * rows, :], g_t[:]).then_inc(gates_stored, 16)
                sp.wait_ge(gates_stored, 16 * b.n + 16)
                sp.wait_ge(hid_ready, TILES * b.n)
                for i in range(2):
                    size = rows // 2 * P
                    src = bass.AP(gates_dram.tensor, (2 * b.n + i) * size, [[0, P], [1, size]])
                    sp.dma_start(gate[i][:].rearrange("p t e n -> p (t e n)"), src).then_inc(gate_loaded[i], 16)

            def scale_out(b):
                sp.wait_ge(result_ready, b.n + 1)
                sp.dma_start(out[b.n].rearrange("(t p) c -> p t c", p=P), f_summed[:]).then_inc(sent, 16)

            each(sp, dict(project_x=project_x, store_parts=store_parts, load_stacks=load_stacks,
                          turn_tau=turn_tau, load_residual=load_residual, turn_gates=turn_gates,
                          scale_out=scale_out))
            sp.wait_ge(sent, 16 * B)

        @block.gpsimd
        def _(pool):
            nc.gpsimd.memset(ident[:], 0.0).then_inc(consts, 1)
            pool.wait_ge(consts, 1)
            nc.gpsimd.affine_select(out=ident[:], in_=ident[:], compare_op=ALU.not_equal, fill=1.0,
                                    base=0, pattern=[[-1, P]], channel_multiplier=1).then_inc(consts, 1)
            nc.gpsimd.memset(mask_q[:], 0.0).then_inc(consts, 1)
            nc.gpsimd.memset(restart[:], 1.0).then_inc(consts, 1)
            pool.wait_ge(consts, 4)
            nc.gpsimd.affine_select(out=mask_q[:], in_=mask_q[:], compare_op=ALU.is_ge, fill=MASKED,
                                    base=T - P, pattern=[[-1, 2 * T - P]],
                                    channel_multiplier=1).then_inc(consts, 1)
            nc.gpsimd.memset(restart[:, :, 0:1], 0.0).then_inc(consts, 1)
            nc.gpsimd.tensor_copy(ident16[:], ident[:]).then_inc(consts, 1)
            nc.gpsimd.memset(minus_half[:], -0.5).then_inc(consts, 1)
            nc.gpsimd.memset(ones_col[:], 1.0).then_inc(consts, 1)
            nc.gpsimd.memset(zeros[:], 0.0).then_inc(consts, 1)
            nc.gpsimd.iota(countdown[:], pattern=[[-1, ROWSETS]], base=ROWSETS, channel_multiplier=0,
                           allow_small_or_imprecise_dtypes=True).then_inc(consts, 1)
            for k in range(2 * TOP):
                last = nc.gpsimd.memset(recip_k[:, k:k + 1], 1.0 / (k + 1))
            last.then_inc(consts, 1)
            for e in range(NE):
                last = nc.gpsimd.memset(order[:, e:e + 1], float(NE - e))
            last.then_inc(consts, 1)

            def project_qk(b, j):
                pool.wait_ge(pre_act, 8 * b.n + 3 + 2 * j)
                nc.gpsimd.tensor_tensor(rest[j][:], rest[j][:], parts[j][:, 0, :], ALU.subtract
                                        ).then_inc(pre_pool, 1)

            def second_parts(b):
                for j in range(2):
                    pool.wait_ge(pre_act, 8 * b.n + 7 + j)
                    nc.gpsimd.tensor_tensor(parts[j][:, 2, :], rest[j][:], parts[j][:, 1, :], ALU.subtract
                                            ).then_inc(pre_pool, 1)

            def turn_tau(b):
                pool.wait_ge(tau_act, 3 * b.n + 2)
                nc.gpsimd.tensor_tensor(tau_rest[:], tau_t[:], tau_parts[:, 0, :], ALU.subtract).then_inc(tau_pool, 1)
                pool.wait_ge(tau_act, 3 * b.n + 3)
                nc.gpsimd.tensor_tensor(tau_parts[:, 2, :], tau_rest[:], tau_parts[:, 1, :],
                                        ALU.subtract).then_inc(tau_pool, 1)

            def pad_v(b):
                if b.n == 0:
                    pool.wait_ge(v_zeroed, 1)
                    pool.wait_ge(loaded, LATER_LOADS * 16)
                pool.wait_ge(av_done, 12 * b.n)
                pool.wait_ge(pre_act, 8 * b.n + 6)
                for r in range(4):
                    dst = v_pad[:].rearrange("p k (j r) c -> p k j r c", r=4)[:, :, :, r, HD * r:HD * r + HD]
                    src = v_nat[b.n % 3][:].rearrange("p k (j r d) -> p k j r d", r=4, d=HD)[:, :, :, r, :]
                    bias = bias_v[:].rearrange("p (j r d) -> p j r d", r=4, d=HD)[:, :, r, :]
                    bias = bias.unsqueeze(1).broadcast_to([P, QT, 4, HD])
                    last = nc.gpsimd.tensor_tensor(dst, src, bias, ALU.add)
                last.then_inc(v_padded, 1)

            def bias_residual(b):
                pool.wait_ge(res_loaded, 16 * b.n + 16)
                nc.gpsimd.tensor_tensor(x_res[:], x_res[:], bias_y[:].unsqueeze(1).broadcast_to([P, QT, C]),
                                        ALU.add).then_inc(res_biased, 1)

            def mask(b, g, blk):
                pool.wait_ge(p_ready, JOBS * b.n + 10 * g + (4, 8, 10)[blk])
                for kt in ((0,), (1, 3), (2,))[blk]:
                    at = T - P if kt == 3 else 0
                    on_diagonal = p_t[blk][:, :, at:at + P]
                    last = nc.gpsimd.affine_select(out=on_diagonal, in_=on_diagonal, compare_op=ALU.is_ge,
                                                   fill=0.0, base=0, pattern=[[0, 4], [1, P]],
                                                   channel_multiplier=-1)
                last.then_inc(p_masked, 1)

            def one_over_deviation(b, step, moments, shifted, minus_mean, var_shifted, rstd, ready):
                pool.wait_ge(step, NORM * b.n + NORM)
                nc.gpsimd.tensor_scalar(shifted[:], moments[:, :, 1], EPS, None, ALU.add).then_inc(var_shifted, 1)
                nc.gpsimd.tensor_scalar(minus_mean[:], moments[:, :, 0], -1.0, None, ALU.mult).then_inc(var_shifted, 1)
                pool.wait_ge(var_shifted, 3 * b.n + 2)
                nc.gpsimd.tensor_tensor(rstd[:], shifted[:], minus_half[:], ALU.pow).then_inc(var_shifted, 1)
                pool.wait_ge(var_shifted, 3 * b.n + 3)
                nc.gpsimd.tensor_tensor(minus_mean[:], minus_mean[:], rstd[:], ALU.mult).then_inc(ready, 1)

            def residual(b):
                one_over_deviation(b, norm_step, moments, shifted, minus_mean, var_shifted, rstd, rstd_ready)

            def sum_out(b):
                one_over_deviation(b, f_norm_step, f_moments, f_shifted, f_minus_mean, f_var_shifted, f_rstd,
                                   f_rstd_ready)

            def up(b, j):
                half, k, h = j // NJ, j % NJ, hid[j % (LAG + 1)]
                if b.n < B - 2:
                    pool.wait_ge(up_act, 2 * TILES * b.n + 2 * j + 2)
                    if b.n or j > LAG:
                        pool.wait_ge(down_done, TILES * b.n + j - LAG)
                    product = nc.gpsimd.tensor_tensor(h[:], silu[j % 2][:], lin[j % 2][:], ALU.mult)
                    product.then_inc(gate_step if k else hid_ready, 1)
                    if k:
                        pool.wait_ge(gate_step, 2 * NE * b.n + half * NE + k)
                else:
                    pool.wait_ge(product_ready, TILES * (b.n - (B - 2)) + j + 1)
                    if k == 0:
                        pool.wait_ge(hid_ready, TILES * b.n + j)
                        pool.sem_inc(hid_ready, 1)
                if k:
                    if k == 1:
                        pool.wait_ge(gate_loaded[half], 16 * b.n + 16)
                    h3 = h[:].rearrange("p (t n) -> p t n", n=P)
                    nc.gpsimd.tensor_tensor(h3, h3, gate[half][:, :, k - 1, :], ALU.mult).then_inc(hid_ready, 1)

            each(pool, dict(project_qk=project_qk, second_parts=second_parts, turn_tau=turn_tau,
                            pad_v=pad_v, bias_residual=bias_residual, mask=mask, residual=residual, sum_out=sum_out,
                            up=up))

        @block.tensor
        def _(pe):
            pe.wait_ge(consts, 2)
            pe.wait_ge(first_loaded, 32)
            pe.sem_inc(s_free, SBANKS)
            pe.sem_inc(fix_done, 1)

            def project_x(b):
                pe.wait_ge(x_loaded, 16 * b.n + 16)
                if b.n:
                    pe.wait_ge(pre_act, 8 * b.n - 2)
                if b.n > 3:
                    pe.wait_ge(o_read, b.n - 3)
                for t in range(QT):
                    last = nc.tensor.transpose(work[:, t * P:(t + 1) * P], x_in[:, t, :], ident[:])
                last.then_inc(pre_ready, 1)

            def project_qk(b, j):
                pe.wait_ge(pre_act, 8 * b.n + 1 + 2 * j)
                nc.tensor.matmul(work[:], w_sb[:, j * C:(j + 1) * C], x_t[:], start=True, stop=True
                                 ).then_inc(pre_ready, 1)

            def project_v(b):
                pe.wait_ge(pre_act, 8 * b.n + 5)
                for t in range(QT):
                    last = nc.tensor.matmul(work[:, t * P:(t + 1) * P], x_t[:, t * P:(t + 1) * P],
                                            w_sb[:, 2 * C:3 * C], start=True, stop=True)
                last.then_inc(pre_ready, 1)

            def scores(b, r):
                p, h, qt = b.p, r // QT, r % QT
                if r == 0:
                    pe.wait_ge(stacks[p], 64 * b.pair + 64)
                    pe.wait_ge(consts, CONSTS)
                    pe.wait_ge(loaded, LATER_LOADS * 16)
                pe.wait_ge(s_free, ROWSETS * b.n + r + 1)
                bank = s_ps[(b.n * ROWSETS + r) % SBANKS]
                w = (qt + 1) * P
                nc.tensor.matmul(bank[:, 0:w], q_st[p][0:KROWS, h * T + qt * P:h * T + qt * P + P],
                                 k_st[p][0:KROWS, h * T:h * T + w], start=True, stop=False)
                nc.tensor.matmul(bank[:, w - P:w], ident16[:], mask_q[:, T - P:T], start=False, stop=True
                                 ).then_inc(s_ready, 1)

            def count_short(b):
                pe.wait_ge(tau_ready, b.n + 1)
                pe.wait_ge(residual_read, b.n)
                nc.tensor.matmul(misc[0:1, 0:ROWSETS], ones_col[:], short[:], start=True, stop=True
                                 ).then_inc(short_counted, 1)

            def fix(b):
                pe.wait_ge(flags_ready, b.n + 1)

                def scores_to_fix(r):
                    p = b.p
                    take_turn(pe, fix_done)
                    pe.wait_ge(y_copied, b.n)
                    nc.tensor.matmul(misc[:], q_st[p][0:KROWS, bass.ds(r * P, P)],
                                     k_st[p][0:KROWS, bass.ds(r // QT * T, T)], start=True, stop=False)
                    nc.tensor.matmul(misc[:], ident16[:], mask_q[:, bass.ds((QT - 1 - r % QT) * P, T)],
                                     start=False, stop=True).then_inc(fix_scores, 1)
                    take_turn(pe, fix_tried)
                    nc.tensor.matmul(y_ps[0:1, 0:1], fix_open[:], ones_col[:], start=True, stop=True
                                     ).then_inc(fix_counted, 1)

                flagged_tiles(pe, scores_to_fix)

            def turn_tau(b):
                pe.wait_ge(tau_final, b.n + 1)
                nc.tensor.transpose(misc[0:ROWSETS, 0:P], neg_tau[:], ident[:]).then_inc(tau_turned, 1)

            def transposed(b, n, g, blk, tiles):
                p = b.p
                if n == 0:
                    pe.wait_ge(tau_rows, 48 * b.n + 48)
                if n == 1 and b.n > 1:
                    pe.wait_ge(o_copied, b.n - 1)
                if b.n or n > 1:
                    pe.wait_ge(p_ready, JOBS * b.n + n - 1)
                bank = t_ps[n % 2]
                col = 0
                for j, kt in tiles:
                    h, w = 4 * j + g, T - kt * P
                    last = nc.tensor.matmul(bank[:, col:col + w], k_st[p][0:KTAU, h * T + kt * P:h * T + kt * P + P],
                                     q_st[p][0:KTAU, h * T + kt * P:h * T + T], start=True, stop=True)
                    col += w
                last.then_inc(t_ready, 1)

            def times_v(b, g, blk):
                pe.wait_ge(p_masked, 12 * b.n + 3 * g + blk + 1)
                if g == 0 and blk == 0:
                    pe.wait_ge(v_padded, b.n + 1)
                    pe.wait_ge(y_copied, b.n)
                for kt in ((0,), (1, 3), (2,))[blk]:
                    w, at = T - kt * P, 3 * P if kt == 3 else 0
                    for j in range(4):
                        last = nc.tensor.matmul(y_ps[32 * j:32 * j + 32, kt * P:T], v_pad[:, kt, 4 * j + g, :],
                                                p_t[blk][:, j, at:at + w],
                                                start=(g == 0 and blk == 0), stop=(g == 3 and blk == 2))
                last.then_inc(av_done, 1)

            def project_y(b):
                pe.wait_ge(y_copied, b.n + 1)
                pe.wait_ge(gates_copied, b.n)
                for t in range(QT):
                    last = nc.tensor.matmul(misc[:, t * P:(t + 1) * P], y_sb[:, t * P:(t + 1) * P], wp_sb[:],
                                            start=True, stop=True)
                last.then_inc(y_projected, 1)

            def turn_x1(b):
                pe.wait_ge(x1_ready, b.n + 1)
                if b.n + 1 < B:
                    pe.wait_ge(tau_act, 3 * (b.n + 1) + 2)
                for t in range(QT):
                    last = nc.tensor.transpose(misc[:, t * P:(t + 1) * P], x1[b.n % 3][:, t, :], ident[:])
                last.then_inc(x1_turned, 1)

            def logits(b):
                pe.wait_ge(x1_copied, b.n + 1)
                for t in range(QT):
                    last = nc.tensor.matmul(misc[:, t * NE:(t + 1) * NE], x1_t[:, t * P:(t + 1) * P], rw[:],
                                            start=True, stop=True)
                last.then_inc(logits_ready, 1)

            def turn_gates(b):
                pe.wait_ge(route_step, ROUTE * b.n + ROUTE)
                nc.tensor.transpose(misc[0:QT * NE, 0:P], gates[:].rearrange("p t e -> p (t e)"), ident[:]
                                    ).then_inc(gates_turned, 1)

            def up(b, j):
                half, k = j // NJ, j % NJ
                if j == 0 and b.n >= B - 2:
                    pe.wait_ge(s_free, ROWSETS * B + SBANKS)
                elif j == 0:
                    pe.wait_ge(o_read, b.n)
                    if b.n + 3 < B:
                        pe.wait_ge(pre_act, 8 * (b.n + 3) + 6)
                if j > 1:
                    pe.wait_ge(up_act, 2 * TILES * b.n + 2 * j - 2)
                bank = banks_of_experts(b)[j % 2]
                xs = x1_t[:, half * HALF:(half + 1) * HALF]
                nc.tensor.matmul(bank[:, 0:HALF], wu[:, k, :], xs, start=True, stop=True)
                nc.tensor.matmul(bank[:, HALF:T], wv[:, k, :], xs, start=True, stop=True).then_inc(up_ready, 1)

            def down(b, j):
                half, k = j // NJ, j % NJ
                pe.wait_ge(hid_ready, TILES * b.n + j + 1)
                if j == 0:
                    pe.wait_ge(o_copied, b.n)
                *_, o_ps = banks_of_experts(b)
                nc.tensor.matmul(o_ps[:, half * HALF:(half + 1) * HALF], wd[:, k, :], hid[j % (LAG + 1)][:],
                                 start=k == 0, stop=k == NJ - 1).then_inc(down_done, 1)

            def turn_out(b):
                pe.wait_ge(o_copied, b.n + 1)
                pe.wait_ge(o_read, b.n)
                for t in range(QT):
                    last = nc.tensor.transpose(work[:, t * P:(t + 1) * P], o_t[:, t * P:(t + 1) * P], ident[:])
                last.then_inc(o_turned, 1)

            each(pe, dict(project_x=project_x, project_qk=project_qk, project_v=project_v, scores=scores,
                          count_short=count_short, fix=fix, turn_tau=turn_tau, transposed=transposed,
                          times_v=times_v, project_y=project_y, turn_x1=turn_x1, logits=logits,
                          turn_gates=turn_gates, up=up, down=down, turn_out=turn_out))

        @block.scalar
        def _(act):
            act.wait_ge(first_loaded, 32)
            nc.scalar.mul(bias_qk[:, 0:1], bias_qk[:, 0:1], SCALE).then_inc(bias_scaled, 1)
            act.wait_ge(bias_scaled, 1)

            def project_x(b):
                act.wait_ge(pre_ready, 4 * b.n + 1)
                nc.scalar.copy(x_t[:], work[:]).then_inc(pre_act, 1)

            def project_qk(b, j):
                act.wait_ge(pre_ready, 4 * b.n + 2 + j)
                if j == 0:
                    act.wait_ge(stored, 96 * b.n)
                scale = SCALE if j == 0 else 1.0
                for dst in (rest[j][:], parts[j][:, 0, :]):
                    nc.scalar.activation(dst, work[:], ACT.Identity, bias=bias_qk[:, j:j + 1], scale=scale
                                         ).then_inc(pre_act, 1)

            def project_v(b):
                act.wait_ge(pre_ready, 4 * b.n + 4)
                if b.n > 2:
                    act.wait_ge(v_padded, b.n - 2)
                nc.scalar.copy(v_nat[b.n % 3][:].rearrange("p t c -> p (t c)"), work[:]).then_inc(pre_act, 1)

            def second_parts(b):
                for j in range(2):
                    act.wait_ge(pre_pool, 4 * b.n + j + 1)
                    nc.scalar.copy(parts[j][:, 1, :], rest[j][:]).then_inc(pre_act, 1)

            def turn_tau(b):
                act.wait_ge(tau_turned, b.n + 1)
                act.wait_ge(tau_pool, 2 * b.n)
                nc.scalar.copy(tau_t[:], misc[0:ROWSETS, 0:P]).then_inc(tau_act, 1)
                act.wait_ge(tau_rows, 48 * b.n)
                nc.scalar.copy(tau_parts[:, 0, :], misc[0:ROWSETS, 0:P]).then_inc(tau_act, 1)
                act.wait_ge(tau_pool, 2 * b.n + 1)
                nc.scalar.copy(tau_parts[:, 1, :], tau_rest[:]).then_inc(tau_act, 1)

            def transposed(b, n, g, blk, tiles):
                if b.n or g:
                    act.wait_ge(av_done, 12 * b.n + 3 * g + blk - 2)
                act.wait_ge(t_ready, JOBS * b.n + n + 1)
                j = tiles[0][0]
                if blk == 2:
                    dst, src = p_t[2][:, j:j + 2, :], t_ps[n % 2][:].rearrange("p (a n) -> p a n", a=2)
                else:
                    dst, src = p_t[blk][:, j, :], t_ps[n % 2][:]
                nc.scalar.activation(dst, src, ACT.Relu).then_inc(p_ready, 1)

            def copy_y(b):
                act.wait_ge(av_done, 12 * b.n + 12)
                act.wait_ge(y_projected, b.n)
                nc.scalar.copy(y_sb[:], y_ps[:]).then_inc(y_copied, 1)

            def turn_x1(b):
                act.wait_ge(x1_turned, b.n + 1)
                act.wait_ge(up_ready, TILES * b.n)
                nc.scalar.copy(x1_t[:], misc[:]).then_inc(x1_copied, 1)

            def softmax(b):
                act.wait_ge(route_step, ROUTE * b.n + 2)
                nc.scalar.activation(score[:], score[:], ACT.Exp).then_inc(exped, 1)

            def turn_gates(b):
                act.wait_ge(gates_turned, b.n + 1)
                act.wait_ge(gates_stored, 16 * b.n)
                nc.scalar.copy(g_t[:], misc[0:QT * NE, 0:P]).then_inc(gates_copied, 1)

            def up(b, j):
                act.wait_ge(up_ready, TILES * b.n + j + 1)
                if b.n or j > 1:
                    act.wait_ge(hid_ready, TILES * b.n + j - 1)
                bank = banks_of_experts(b)[j % 2]
                nc.scalar.activation(silu[j % 2][:], bank[:, 0:HALF], ACT.Silu).then_inc(up_act, 1)
                nc.scalar.copy(lin[j % 2][:], bank[:, HALF:T]).then_inc(up_act, 1)

            def normalise(dst, src, minus_mean, rstd, ready):
                for t in range(QT):
                    last = nc.scalar.activation(dst[:, t, :], src[:, t, :], ACT.Identity,
                                                bias=minus_mean[:, t:t + 1], scale=rstd[:, t:t + 1])
                last.then_inc(ready, 1)

            def scale_x1(b):
                act.wait_ge(rstd_ready, b.n + 1)
                if b.n > 2:
                    act.wait_ge(o_read, b.n - 2)
                normalise(x1[b.n % 3], summed, minus_mean, rstd, x1_ready)

            def scale_out(b):
                act.wait_ge(f_rstd_ready, b.n + 1)
                normalise(f_summed, f_summed, f_minus_mean, f_rstd, result_ready)

            def copy_out(b):
                *_, o_ps = banks_of_experts(b)
                act.wait_ge(down_done, TILES * b.n + TILES)
                act.wait_ge(o_turned, b.n)
                nc.scalar.copy(o_t[:], o_ps[:]).then_inc(o_copied, 1)

            each(act, dict(project_x=project_x, project_qk=project_qk, project_v=project_v,
                           second_parts=second_parts, turn_tau=turn_tau, transposed=transposed,
                           scale_x1=scale_x1, scale_out=scale_out, copy_y=copy_y, turn_x1=turn_x1,
                           softmax=softmax, turn_gates=turn_gates, up=up,
                           copy_out=copy_out))

        @block.vector
        def _(dve):
            for i in range(2):
                nc.vector.memset(k_st[i][64:96, :], 1.0).then_inc(rows_of_ones, 1)
            nc.vector.memset(v_pad[:], 0.0).then_inc(v_zeroed, 1)
            nc.vector.memset(top[:, 0:ROWSETS:QT, CH - 1, :], MASKED)
            dve.wait_ge(consts, CONSTS)
            dve.wait_ge(loaded, LATER_LOADS * 16)

            def chain(sem, b, per):
                n = [0]

                def link(ins):
                    n[0] += 1
                    assert n[0] <= per
                    ins.then_inc(sem, 1)
                    dve.wait_ge(sem, per * b.n + n[0])
                return link

            def scores(b, r):
                dve.wait_ge(s_ready, ROWSETS * b.n + r + 1)
                w = (r % QT + 1) * P
                count = CH if r % QT else CH - 1
                for k in range(count):
                    last = nc.vector.max(top[:, r, k, :], s_ps[(b.n * ROWSETS + r) % SBANKS][:, k:w:count])
                last.then_inc(s_free, 1)

            def by_rows(ap):
                return ap.rearrange("p (r i) -> p r i", i=2 * TOP)

            def every_row(table):
                return table[:].unsqueeze(1).broadcast_to([P, ROWSETS, 2 * TOP])

            def thresholds(b):
                link = chain(sort_step, b, SORT)
                dve.wait_ge(s_free, ROWSETS * b.n + SBANKS + ROWSETS)

                def exchange(dst, src, size, stride, count):
                    s = src[:, 0:count].rearrange("p (g a s) -> p g a s", a=2, s=stride)
                    d = dst[:, 0:count].rearrange("p (g a s) -> p g a s", a=2, s=stride)
                    nc.vector.tensor_tensor(d[:, :, 0, :], s[:, :, 0, :], s[:, :, 1, :], ALU.max)
                    link(nc.vector.tensor_tensor(d[:, :, 1, :], s[:, :, 0, :], s[:, :, 1, :], ALU.min))

                pairs = top[:].rearrange("p r (m a) i -> p (r m) a i", a=2)
                merged = m_a[:].rearrange("p (g a i) -> p g a i", a=2, i=TOP)
                nc.vector.tensor_tensor(merged[:, :, 0, :], pairs[:, :, 0, :], pairs[:, :, 1, ::-1], ALU.max)
                link(nc.vector.tensor_tensor(merged[:, :, 1, :], pairs[:, :, 0, :], pairs[:, :, 1, ::-1], ALU.min))
                exchange(m_b, m_a, TOP, 4, ROWSETS * CH * TOP)
                exchange(m_a, m_b, TOP, 2, ROWSETS * CH * TOP)
                exchange(m_b, m_a, TOP, 1, ROWSETS * CH * TOP)
                two = m_b[:].rearrange("p (r m i) -> p r m i", m=2, i=2 * TOP)
                kept = ROWSETS * 2 * TOP
                link(nc.vector.tensor_tensor(m_a[:, 0:kept].rearrange("p (r i) -> p r i", i=2 * TOP),
                                             two[:, :, 0, :], two[:, :, 1, ::-1], ALU.max))
                exchange(m_b, m_a, 2 * TOP, 8, kept)
                exchange(m_a, m_b, 2 * TOP, 4, kept)
                exchange(m_b, m_a, 2 * TOP, 2, kept)
                exchange(m_a, m_b, 2 * TOP, 1, kept)
                ranked = m_a[:, 0:kept]
                prefix = m_b[:, 0:kept]
                link(nc.vector.tensor_tensor_scan(prefix, restart[:].rearrange("p r i -> p (r i)"), ranked, 0.0,
                                                  ALU.mult, ALU.add))
                link(nc.vector.scalar_tensor_tensor(out=by_rows(prefix), in0=by_rows(prefix), scalar=1.0,
                                                    in1=every_row(recip_k), op0=ALU.subtract, op1=ALU.mult))
                nc.vector.tensor_reduce(tau[:], prefix.rearrange("p (r i) -> p r i", i=2 * TOP), AX, ALU.max)
                link(nc.vector.tensor_reduce(last_kept[:], top[:, :, :, TOP - 1], AX, ALU.max))
                link(nc.vector.tensor_tensor(last_kept[:], last_kept[:],
                                             ranked.rearrange("p (r i) -> p r i", i=2 * TOP)[:, :, 2 * TOP - 1],
                                             ALU.max))
                nc.vector.tensor_tensor(short[:], last_kept[:], tau[:], ALU.is_gt).then_inc(tau_ready, 1)

            def flags(b):
                link = chain(flag_step, b, 3)
                dve.wait_ge(short_counted, b.n + 1)
                dve.wait_ge(tau_ready, b.n + 1)
                link(nc.vector.tensor_scalar(short_any[:], misc[0:1, 0:ROWSETS], 0.5, None, ALU.is_gt))
                nc.vector.tensor_copy(short_i[:], short_any[:])
                nc.vector.tensor_tensor(from_end[:], short_any[:], countdown[:], ALU.mult)
                link(nc.vector.tensor_reduce(total[:], short_any[:], AX, ALU.add))
                nc.vector.tensor_scalar(plan_i[0:1, 0:1], total[:], float(TOP), None, ALU.min)
                nc.vector.tensor_scalar(plan_i[0:1, 1:2], total[:], float(TOP), None, ALU.is_gt)
                link(nc.vector.max(first_few[:], from_end[:]))
                nc.vector.tensor_scalar(list_i[:], first_few[:], -1.0, float(ROWSETS), ALU.mult, ALU.add
                                        ).then_inc(flags_ready, 1)
                dve.wait_ge(flags_ready, b.n + 1)

            def newton_step():
                nc.vector.scalar_tensor_tensor(out=fix_over[:], in0=misc[:], scalar=fix_tau[:, 0:1], in1=zeros[:],
                                               op0=ALU.subtract, op1=ALU.max, accum_out=fix_sum[:, 0:1])
                nc.vector.tensor_scalar(fix_over2[:], misc[:], fix_tau[:, 0:1], 0.0,
                                        ALU.is_gt, ALU.add, accum_out=fix_sum[:, 1:2])
                dve.drain()
                nc.vector.reciprocal(fix_sum[:, 1:2], fix_sum[:, 1:2])
                nc.vector.tensor_scalar(fix_sum[:, 0:1], fix_sum[:, 0:1], 1.0, None, ALU.subtract)
                dve.drain()
                nc.vector.scalar_tensor_tensor(out=fix_tau[:], in0=fix_sum[:, 0:1], scalar=fix_sum[:, 1:2],
                                               in1=fix_tau[:], op0=ALU.mult, op1=ALU.add)
                dve.drain()

            def fix(r):
                nc.vector.tensor_copy(fix_tau[:], tau[:, bass.ds(r, 1)])
                take_turn(dve, fix_scores)
                dve.drain()
                for _ in range(FEW):
                    newton_step()
                nc.vector.tensor_scalar(fix_open[:], fix_sum[:, 0:1], CLOSE, None, ALU.is_gt
                                        ).then_inc(fix_tried, 1)
                take_turn(dve, fix_counted)
                nc.vector.tensor_copy(open_i[:], y_ps[0:1, 0:1])
                dve.drain()
                still = dve.value_load(open_i[0:1, 0:1], min_val=0, max_val=P)
                with dve.If(still):
                    with dve.Fori(0, NEWTON - FEW):
                        newton_step()
                nc.vector.tensor_copy(tau[:, bass.ds(r, 1)], fix_tau[:]).then_inc(fix_done, 1)
                dve.drain()

            def fix_thresholds(b):
                flagged_tiles(dve, fix)
                nc.vector.tensor_scalar(neg_tau[:], tau[:], -1.0, None, ALU.mult).then_inc(tau_final, 1)

            def normalise_moments(link, total, stats, moments):
                for t in range(QT):
                    last = nc.vector.bn_stats(stats[:, t, :], total[:, t, :])
                link(last)
                for t in range(QT):
                    last = nc.vector.bn_aggr(moments[:, t, :], stats[:, t, :])
                link(last)

            def residual(b):
                dve.wait_ge(y_projected, b.n + 1)
                dve.wait_ge(res_biased, b.n + 1)
                dve.wait_ge(x1_ready, b.n)
                nc.vector.tensor_tensor(summed[:], misc[:].rearrange("p (t c) -> p t c", c=C), x_res[:],
                                        ALU.add).then_inc(residual_read, 1)
                dve.wait_ge(residual_read, b.n + 1)
                normalise_moments(chain(norm_step, b, NORM), summed, stats, moments)

            logits_ps = misc[:, 0:QT * NE].rearrange("p (t e) -> p t e", e=NE)

            def over_experts(ap):
                return ap.unsqueeze(2).broadcast_to([P, QT, NE])

            def over_tiles(ap):
                return ap.unsqueeze(1).broadcast_to([P, QT, NE])

            def route(b, step):
                dve.wait_ge(route_step, ROUTE * b.n + step)
                if step == 0:
                    dve.wait_ge(logits_ready, b.n + 1)
                    ins = nc.vector.tensor_reduce(most[:], logits_ps, AX, ALU.max)
                elif step == 1:
                    ins = nc.vector.tensor_tensor(score[:], logits_ps, over_experts(most[:]), ALU.subtract)
                elif step == 2:
                    dve.wait_ge(exped, b.n + 1)
                    ins = nc.vector.tensor_reduce(most[:], score[:], AX, ALU.add)
                elif step == 3:
                    ins = nc.vector.reciprocal(most[:], most[:])
                elif step == 4:
                    ins = nc.vector.tensor_tensor(score[:], score[:], over_experts(most[:]), ALU.mult)
                elif step == 5:
                    ins = nc.vector.tensor_tensor(biased[:], score[:], over_tiles(bias_e[:]), ALU.add)
                elif step in (6, 12):
                    ins = nc.vector.tensor_reduce(most[:], biased[:], AX, ALU.max)
                elif step in (7, 13):
                    ins = nc.vector.tensor_tensor(equal[:], biased[:], over_experts(most[:]), ALU.is_equal)
                elif step in (8, 14):
                    ins = nc.vector.tensor_tensor(equal[:], equal[:], over_tiles(order[:]), ALU.mult)
                elif step in (9, 15):
                    ins = nc.vector.tensor_reduce(most[:], equal[:], AX, ALU.max)
                elif step in (10, 16):
                    ins = nc.vector.tensor_tensor(chosen[step // 16][:], equal[:], over_experts(most[:]),
                                                  ALU.is_equal)
                elif step == 11:
                    ins = nc.vector.scalar_tensor_tensor(out=biased[:], in0=chosen[0][:], scalar=MASKED,
                                                         in1=biased[:], op0=ALU.mult, op1=ALU.add)
                elif step == 17:
                    ins = nc.vector.tensor_tensor(gates[:], chosen[0][:], chosen[1][:], ALU.add)
                else:
                    ins = nc.vector.tensor_tensor(gates[:], gates[:], score[:], ALU.mult)
                ins.then_inc(route_step, 1)

            def sum_out(b):
                dve.wait_ge(o_turned, b.n + 1)
                dve.wait_ge(sent, 16 * b.n)
                nc.vector.tensor_tensor(f_summed[:], work[:].rearrange("p (t c) -> p t c", c=C), x1[b.n % 3][:],
                                        ALU.add).then_inc(o_read, 1)
                dve.wait_ge(o_read, b.n + 1)
                normalise_moments(chain(f_norm_step, b, NORM), f_summed, f_stats, f_moments)

            def up(b, j):
                if b.n >= B - 2:
                    dve.wait_ge(up_act, 2 * TILES * b.n + 2 * j + 2)
                    dve.wait_ge(down_done, TILES * b.n + j - LAG)
                    product = nc.vector.tensor_tensor(hid[j % (LAG + 1)][:], silu[j % 2][:], lin[j % 2][:], ALU.mult)
                    product.then_inc(product_ready, 1)

            each(dve, dict(scores=scores, sort=thresholds, flags=flags, fix=fix_thresholds, residual=residual,
                           route=route, sum_out=sum_out, up=up))


_INS = ["L0_attn_x", "L0_attn_w_attn", "L0_attn_b_attn", "L0_attn_w_proj", "L0_attn_b_proj",
        "L0_ffn_router_w", "L0_ffn_expert_bias", "L0_ffn_w1", "L0_ffn_w2", "L0_ffn_w3",
        "L0_ffn_sw1", "L0_ffn_sw2", "L0_ffn_sw3"]


def kernel(**inputs):
    import numpy as _np
    import concourse.bacc as _bacc
    from concourse import mybir as _mybir
    from concourse.bass_utils import run_bass_kernel_spmd as _run

    nc = _bacc.Bacc("TRN2", target_bir_lowering=False, num_devices=1)
    arrays, args = {}, []
    for name in _INS:
        a = _np.ascontiguousarray(inputs[name])
        arrays[f"in_{name}"] = a
        args.append(nc.dram_tensor(f"in_{name}", a.shape, _mybir.dt.from_np(a.dtype), kind="ExternalInput").ap())
    args.append(nc.dram_tensor("out_0", (B, T, C), _mybir.dt.float32, kind="ExternalOutput").ap())
    program(nc, *args)
    r = _run(nc, [arrays], core_ids=[0])
    return r.results[0]["out_0"]
```
